# Optimizing a Trainium2 kernel written in Bass

```python
import numpy as np
import jax
import jax.numpy as jnp

def _softmax(x, axis=-1):
    return jax.nn.softmax(x, axis=axis)

def _gelu(x):
    return jax.nn.gelu(x, approximate=True)

def _silu(x):
    return jax.nn.silu(x)

def _sigmoid(x):
    return jax.nn.sigmoid(x)

def _layernorm(x, axis=-1, eps=1e-05):
    m = jnp.mean(x, axis=axis, keepdims=True)
    v = jnp.var(x, axis=axis, keepdims=True)
    return (x - m) / jnp.sqrt(v + eps)

def _scatter_add(tgt, idx, src, axis=0):
    return tgt.at[idx].add(src)

def _segment_sum(src, seg, n):
    return jax.ops.segment_sum(src, seg, n)
kernel_name = 'mk_xattn_ffn_d2_seqx_r8_cdadc8'

def setup_inputs(seed: int=0):
    np.random.seed(seed)
    _w = jnp.asarray

    def _rec_inputs():
        import jax
        import jax.numpy as jnp
        _rk = jax.random.key(seed)
        x = -0.0005207 + 1.001 * jax.random.normal(jax.random.fold_in(_rk, 1), (4, 256, 256), jnp.float32)
        _lenS = 256 - jax.random.randint(jax.random.fold_in(_rk, 7), (4,), 0, max(1, 256 // 4) + 1, jnp.int32)
        _lenS2 = 1601 - jax.random.randint(jax.random.fold_in(_rk, 8), (4,), 0, max(1, 1601 // 4) + 1, jnp.int32)
        _ctx_2048P = jax.random.normal(jax.random.fold_in(_rk, 12), (4, 16, 256), jnp.float32)
        _ctx_2048c = jax.random.dirichlet(jax.random.fold_in(_rk, 512), 0.3 * jnp.ones((16,), jnp.float32), (4, 1601))
        _ctx_2048t = jnp.einsum('bsk,bkd->bsd', _ctx_2048c, _ctx_2048P)
        _ctx_2048t = _ctx_2048t * jax.lax.rsqrt(jnp.mean(jnp.square(_ctx_2048t)) + 1e-12) * 0.953939
        ctx_2048 = -5.72187e-05 + 0.999849 * (_ctx_2048t + 0.3 * jax.random.normal(jax.random.fold_in(_rk, 612), (4, 1601, 256), jnp.float32))
        _validS = jnp.arange(256)[None, :] < _lenS[:, None]
        _validS2 = jnp.arange(1601)[None, :] < _lenS2[:, None]
        _causal = jnp.tril(jnp.ones((256, 256), dtype=bool))
        mask_BxSx4224_bf0 = jnp.logical_not(jnp.ones((4, 256, 528), dtype=bool))
        return (x, ctx_2048, mask_BxSx4224_bf0)
    x, ctx_2048, mask_BxSx4224_bf0 = _rec_inputs()

    def _L0_xattn_setup():
        import jax, jax.numpy as jnp
        import numpy as np
        import math
        DIM = 256
        B, Q_LEN, KV_LEN = (8, 128, 512)
        key = jax.random.key(seed)
        ks = jax.random.split(key, 8)
        x = jax.random.normal(ks[0], (B, Q_LEN, DIM), dtype=jnp.float32)
        mask = jnp.zeros((B, Q_LEN, KV_LEN + Q_LEN), dtype=bool)
        k_cache = jax.random.normal(ks[1], (B, KV_LEN, DIM), dtype=jnp.float32)
        v_cache = jax.random.normal(ks[2], (B, KV_LEN, DIM), dtype=jnp.float32)
        scale = 1.0 / math.sqrt(DIM)
        wq = jax.random.normal(ks[3], (DIM, DIM), dtype=jnp.float32) * scale
        wk = jax.random.normal(ks[4], (DIM, DIM), dtype=jnp.float32) * scale
        wv = jax.random.normal(ks[5], (DIM, DIM), dtype=jnp.float32) * scale
        wo = jax.random.normal(ks[6], (DIM, DIM), dtype=jnp.float32) * scale
        return {'x': x, 'mask': mask, 'k_cache': k_cache, 'v_cache': v_cache, 'wq': wq, 'wk': wk, 'wv': wv, 'wo': wo}
    _L0_xattn_all = _L0_xattn_setup()
    _L0_xattn_in = {k: v for k, v in _L0_xattn_all.items() if k in ('wq', 'wk', 'wv', 'wo')}
    del _L0_xattn_all

    def _L0_ffn_setup():
        import jax, jax.numpy as jnp
        import numpy as np
        HIDDEN = 256
        NUM_EXPERTS = 32
        TOP_K = 4
        MOE_INTER = 96
        GROUP = 2
        NUM_CHUNK = NUM_EXPERTS // GROUP
        CHUNK_INTER = 128
        SMALL_SCALE = 0.05

        def _routing(x2d, gate_w):
            logits = x2d @ gate_w.T
            rw = jax.nn.softmax(logits.astype(jnp.float32), axis=-1)
            scores = jax.nn.sigmoid(logits.astype(jnp.float32))
            _, sel = jax.lax.top_k(scores, TOP_K)
            w = jnp.take_along_axis(rw, sel, axis=-1)
            w = w / w.sum(axis=-1, keepdims=True)
            return (w.astype(x2d.dtype), sel)

        def _moe(x2d, Wg, Wu, Wd, cw):
            g = jnp.einsum('th,ehi->eti', x2d, Wg)
            u = jnp.einsum('th,ehi->eti', x2d, Wu)
            a = jax.nn.silu(g) * u * cw.T[:, :, None]
            return jnp.einsum('eti,eih->th', a, Wd)
        key = jax.random.key(seed)
        ks = jax.random.split(key, 8)
        s = 0.02
        B, S = (2, 256)
        return {'hidden_states': jax.random.normal(ks[0], (B, S, HIDDEN), jnp.float32), 'gate_w': jax.random.normal(ks[1], (NUM_EXPERTS, HIDDEN), jnp.float32) * s, 'Wg': jax.random.normal(ks[2], (NUM_EXPERTS, HIDDEN, MOE_INTER), jnp.float32) * s, 'Wu': jax.random.normal(ks[3], (NUM_EXPERTS, HIDDEN, MOE_INTER), jnp.float32) * s, 'Wd': jax.random.normal(ks[4], (NUM_EXPERTS, MOE_INTER, HIDDEN), jnp.float32) * s, 'cWg': jax.random.normal(ks[5], (NUM_CHUNK, HIDDEN, CHUNK_INTER), jnp.float32) * s, 'cWu': jax.random.normal(ks[6], (NUM_CHUNK, HIDDEN, CHUNK_INTER), jnp.float32) * s, 'cWd': jax.random.normal(ks[7], (NUM_CHUNK, CHUNK_INTER, HIDDEN), jnp.float32) * s}
    _L0_ffn_all = _L0_ffn_setup()
    _L0_ffn_in = {k: v for k, v in _L0_ffn_all.items() if k in ('gate_w', 'Wg', 'Wu', 'Wd', 'cWg', 'cWu', 'cWd')}
    del _L0_ffn_all

    def _L1_xattn_setup():
        import jax, jax.numpy as jnp
        import numpy as np
        HIDDEN = 256
        N_HEADS = 16
        N_KV_HEADS = 4
        HEAD_DIM = 128
        EPS = 1e-06

        def rms_norm(x, w, eps=EPS):
            xf = x.astype(jnp.float32)
            var = jnp.mean(xf * xf, axis=-1, keepdims=True)
            return w * (xf * jax.lax.rsqrt(var + eps)).astype(x.dtype)
        key = jax.random.key(seed)
        ks = jax.random.split(key, 8)
        B, S, S_ENC = (4, 256, 128)
        inner = N_HEADS * HEAD_DIM
        kv_dim = N_KV_HEADS * HEAD_DIM
        s = 0.02
        return {'hidden_states': jax.random.normal(ks[0], (B, S, HIDDEN), jnp.float32), 'encoder_hidden_states': jax.random.normal(ks[1], (B, S_ENC, HIDDEN), jnp.float32), 'Wq': jax.random.normal(ks[2], (HIDDEN, inner), jnp.float32) * s, 'Wk': jax.random.normal(ks[3], (HIDDEN, kv_dim), jnp.float32) * s, 'Wv': jax.random.normal(ks[4], (HIDDEN, kv_dim), jnp.float32) * s, 'Wo': jax.random.normal(ks[5], (inner, HIDDEN), jnp.float32) * s, 'q_norm_w': jnp.ones((HEAD_DIM,), jnp.float32), 'k_norm_w': jnp.ones((HEAD_DIM,), jnp.float32)}
    _L1_xattn_all = _L1_xattn_setup()
    _L1_xattn_in = {k: v for k, v in _L1_xattn_all.items() if k in ('Wq', 'Wk', 'Wv', 'Wo', 'q_norm_w', 'k_norm_w')}
    del _L1_xattn_all

    def _L1_ffn_setup():
        import jax, jax.numpy as jnp
        import numpy as np
        EPS = 1e-05
        RMS_EPS = 1e-06

        def activation_quant(x, num_bits=8):
            qn = -2 ** (num_bits - 1)
            qp = 2 ** (num_bits - 1) - 1
            xf = x.astype(jnp.float32)
            s = qp / jnp.clip(jnp.max(jnp.abs(xf), axis=-1, keepdims=True), EPS, None)
            return (jnp.clip(jnp.round(xf * s), qn, qp) / s).astype(x.dtype)

        def weight_quant(w):
            wf = w.astype(jnp.float32)
            s = 1.0 / jnp.clip(jnp.mean(jnp.abs(wf)), EPS, None)
            return (jnp.clip(jnp.round(wf * s), -1.0, 1.0) / s).astype(w.dtype)

        def bit_linear(x, w):
            qx = x + jax.lax.stop_gradient(activation_quant(x) - x)
            qw = w + jax.lax.stop_gradient(weight_quant(w) - w)
            return jnp.einsum('bsh,oh->bso', qx, qw)

        def rms_norm(x, weight, eps=RMS_EPS):
            xf = x.astype(jnp.float32)
            var = jnp.mean(xf * xf, axis=-1, keepdims=True)
            return weight * (xf * jax.lax.rsqrt(var + eps)).astype(x.dtype)
        key = jax.random.key(seed)
        k1, k2, k3, k4 = jax.random.split(key, 4)
        B, S, H, I = (2, 256, 256, 1024)
        scale = 1.0 / np.sqrt(H)
        return {'x': jax.random.normal(k1, (B, S, H), dtype=jnp.float32), 'w_gate': jax.random.normal(k2, (I, H), dtype=jnp.float32) * scale, 'w_up': jax.random.normal(k3, (I, H), dtype=jnp.float32) * scale, 'w_down': jax.random.normal(k4, (H, I), dtype=jnp.float32) * (1.0 / np.sqrt(I)), 'ln_weight': jnp.ones((I,), dtype=jnp.float32)}
    _L1_ffn_all = _L1_ffn_setup()
    _L1_ffn_in = {k: v for k, v in _L1_ffn_all.items() if k in ('w_gate', 'w_up', 'w_down', 'ln_weight')}
    del _L1_ffn_all
    return {'x': x, 'ctx_2048': ctx_2048, 'mask_BxSx4224_bf0': mask_BxSx4224_bf0, 'L0_xattn_wq': _L0_xattn_in['wq'], 'L0_xattn_wk': _L0_xattn_in['wk'], 'L0_xattn_wv': _L0_xattn_in['wv'], 'L0_xattn_wo': _L0_xattn_in['wo'], 'L0_ffn_gate_w': _L0_ffn_in['gate_w'], 'L0_ffn_Wg': _L0_ffn_in['Wg'], 'L0_ffn_Wu': _L0_ffn_in['Wu'], 'L0_ffn_Wd': _L0_ffn_in['Wd'], 'L0_ffn_cWg': _L0_ffn_in['cWg'], 'L0_ffn_cWu': _L0_ffn_in['cWu'], 'L0_ffn_cWd': _L0_ffn_in['cWd'], 'L1_xattn_Wq': _L1_xattn_in['Wq'], 'L1_xattn_Wk': _L1_xattn_in['Wk'], 'L1_xattn_Wv': _L1_xattn_in['Wv'], 'L1_xattn_Wo': _L1_xattn_in['Wo'], 'L1_xattn_q_norm_w': _L1_xattn_in['q_norm_w'], 'L1_xattn_k_norm_w': _L1_xattn_in['k_norm_w'], 'L1_ffn_w_gate': _L1_ffn_in['w_gate'], 'L1_ffn_w_up': _L1_ffn_in['w_up'], 'L1_ffn_w_down': _L1_ffn_in['w_down'], 'L1_ffn_ln_weight': _L1_ffn_in['ln_weight']}

def reference(x, ctx_2048, mask_BxSx4224_bf0, L0_xattn_wq, L0_xattn_wk, L0_xattn_wv, L0_xattn_wo, L0_ffn_gate_w, L0_ffn_Wg, L0_ffn_Wu, L0_ffn_Wd, L0_ffn_cWg, L0_ffn_cWu, L0_ffn_cWd, L1_xattn_Wq, L1_xattn_Wk, L1_xattn_Wv, L1_xattn_Wo, L1_xattn_q_norm_w, L1_xattn_k_norm_w, L1_ffn_w_gate, L1_ffn_w_up, L1_ffn_w_down, L1_ffn_ln_weight):
    import jax
    import jax.numpy as jnp

    def _L0_xattn_ref(x, mask, k_cache, v_cache, wq, wk, wv, wo):
        import jax, jax.numpy as jnp
        import numpy as np
        import math
        DIM = 256
        B, Q_LEN, KV_LEN = (8, 128, 512)
        q = jnp.einsum('bsd,ed->bse', x, wq)
        k_new = jnp.einsum('bsd,ed->bse', x, wk)
        v_new = jnp.einsum('bsd,ed->bse', x, wv)
        k = jnp.concatenate([k_cache, k_new], axis=1)
        v = jnp.concatenate([v_cache, v_new], axis=1)
        scale = 1.0 / math.sqrt(q.shape[-1])
        scores = jnp.einsum('bqd,bkd->bqk', q, k) * scale
        attn = jax.nn.softmax(scores, axis=-1)
        out = jnp.einsum('bqk,bkd->bqd', attn, v)
        return jnp.einsum('bqd,ed->bqe', out, wo)

    def _L0_ffn_ref(hidden_states, gate_w, Wg, Wu, Wd, cWg, cWu, cWd):
        import jax, jax.numpy as jnp
        import numpy as np
        HIDDEN = 256
        NUM_EXPERTS = 32
        TOP_K = 4
        MOE_INTER = 96
        GROUP = 2
        NUM_CHUNK = NUM_EXPERTS // GROUP
        CHUNK_INTER = 128
        SMALL_SCALE = 0.05

        def _routing(x2d, gate_w):
            logits = x2d @ gate_w.T
            rw = jax.nn.softmax(logits.astype(jnp.float32), axis=-1)
            scores = jax.nn.sigmoid(logits.astype(jnp.float32))
            _, sel = jax.lax.top_k(scores, TOP_K)
            w = jnp.take_along_axis(rw, sel, axis=-1)
            w = w / w.sum(axis=-1, keepdims=True)
            return (w.astype(x2d.dtype), sel)

        def _moe(x2d, Wg, Wu, Wd, cw):
            g = jnp.einsum('th,ehi->eti', x2d, Wg)
            u = jnp.einsum('th,ehi->eti', x2d, Wu)
            a = jax.nn.silu(g) * u * cw.T[:, :, None]
            return jnp.einsum('eti,eih->th', a, Wd)
        B, S, H = hidden_states.shape
        T = B * S
        x = hidden_states.reshape(T, H)
        w, sel = _routing(x, gate_w)
        rows = jnp.arange(T)[:, None]
        cw_large = jnp.zeros((T, NUM_EXPERTS), x.dtype).at[rows, sel].add(w)
        cw_small = jnp.zeros((T, NUM_CHUNK), x.dtype).at[rows, sel // GROUP].add(w)
        large = _moe(x, Wg, Wu, Wd, cw_large)
        small = _moe(x, cWg, cWu, cWd, cw_small)
        return (large + SMALL_SCALE * small).reshape(B, S, H)

    def _L1_xattn_ref(hidden_states, encoder_hidden_states, Wq, Wk, Wv, Wo, q_norm_w, k_norm_w):
        import jax, jax.numpy as jnp
        import numpy as np
        HIDDEN = 256
        N_HEADS = 16
        N_KV_HEADS = 4
        HEAD_DIM = 128
        EPS = 1e-06

        def rms_norm(x, w, eps=EPS):
            xf = x.astype(jnp.float32)
            var = jnp.mean(xf * xf, axis=-1, keepdims=True)
            return w * (xf * jax.lax.rsqrt(var + eps)).astype(x.dtype)
        B, S, _ = hidden_states.shape
        S_enc = encoder_hidden_states.shape[1]
        groups = N_HEADS // N_KV_HEADS
        scale = 1.0 / HEAD_DIM ** 0.5
        q = (hidden_states @ Wq).reshape(B, S, N_HEADS, HEAD_DIM)
        k = (encoder_hidden_states @ Wk).reshape(B, S_enc, N_KV_HEADS, HEAD_DIM)
        v = (encoder_hidden_states @ Wv).reshape(B, S_enc, N_KV_HEADS, HEAD_DIM)
        q = rms_norm(q, q_norm_w)
        k = rms_norm(k, k_norm_w)
        k = jnp.repeat(k, groups, axis=2)
        v = jnp.repeat(v, groups, axis=2)
        scores = jnp.einsum('bqhd,bkhd->bhqk', q, k) * scale
        probs = jax.nn.softmax(scores, axis=-1)
        out = jnp.einsum('bhqk,bkhd->bqhd', probs, v)
        out = out.reshape(B, S, N_HEADS * HEAD_DIM)
        return out @ Wo

    def _L1_ffn_ref(x, w_gate, w_up, w_down, ln_weight):
        import jax, jax.numpy as jnp
        import numpy as np
        EPS = 1e-05
        RMS_EPS = 1e-06

        def activation_quant(x, num_bits=8):
            qn = -2 ** (num_bits - 1)
            qp = 2 ** (num_bits - 1) - 1
            xf = x.astype(jnp.float32)
            s = qp / jnp.clip(jnp.max(jnp.abs(xf), axis=-1, keepdims=True), EPS, None)
            return (jnp.clip(jnp.round(xf * s), qn, qp) / s).astype(x.dtype)

        def weight_quant(w):
            wf = w.astype(jnp.float32)
            s = 1.0 / jnp.clip(jnp.mean(jnp.abs(wf)), EPS, None)
            return (jnp.clip(jnp.round(wf * s), -1.0, 1.0) / s).astype(w.dtype)

        def bit_linear(x, w):
            qx = x + jax.lax.stop_gradient(activation_quant(x) - x)
            qw = w + jax.lax.stop_gradient(weight_quant(w) - w)
            return jnp.einsum('bsh,oh->bso', qx, qw)

        def rms_norm(x, weight, eps=RMS_EPS):
            xf = x.astype(jnp.float32)
            var = jnp.mean(xf * xf, axis=-1, keepdims=True)
            return weight * (xf * jax.lax.rsqrt(var + eps)).astype(x.dtype)
        h = jax.nn.silu(bit_linear(x, w_gate)) * bit_linear(x, w_up)
        h = rms_norm(h, ln_weight)
        return bit_linear(h, w_down)
    x = x + _L0_xattn_ref(_layernorm(x, axis=-1), mask_BxSx4224_bf0, ctx_2048, ctx_2048, L0_xattn_wq, L0_xattn_wk, L0_xattn_wv, L0_xattn_wo)
    x = x + _L0_ffn_ref(_layernorm(x, axis=-1), L0_ffn_gate_w, L0_ffn_Wg, L0_ffn_Wu, L0_ffn_Wd, L0_ffn_cWg, L0_ffn_cWu, L0_ffn_cWd)
    x = x + _L1_xattn_ref(_layernorm(x, axis=-1), ctx_2048, L1_xattn_Wq, L1_xattn_Wk, L1_xattn_Wv, L1_xattn_Wo, L1_xattn_q_norm_w, L1_xattn_k_norm_w)
    x = x + _L1_ffn_ref(_layernorm(x, axis=-1), L1_ffn_w_gate, L1_ffn_w_up, L1_ffn_w_down, L1_ffn_ln_weight)
    return x

_drawn_inputs = setup_inputs


def setup_inputs(seed=0):
    import zlib

    import numpy as np

    out = dict(_drawn_inputs(seed))
    spreads = {'L1_xattn_q_norm_w': (1.0, 0.6),
     'L1_xattn_k_norm_w': (1.0, 0.6),
     'L1_ffn_ln_weight': (1.0, 0.2)}
    factors = {'L0_ffn_gate_w': 4.496,
     'L0_ffn_Wg': 4.411,
     'L0_ffn_Wu': 4.348,
     'L0_ffn_Wd': 4.376,
     'L0_ffn_cWg': 8.0,
     'L0_ffn_cWu': 8.0,
     'L0_ffn_cWd': 8.0}
    for name, (base, spread) in spreads.items():
        noise = np.random.default_rng([zlib.crc32(name.encode()), seed]).standard_normal(out[name].shape)
        drawn = base * np.exp(spread * noise) if base else spread * noise
        out[name] = jnp.asarray(drawn.astype(out[name].dtype))
    for name, factor in factors.items():
        out[name] = (out[name] * factor).astype(out[name].dtype)
    return out
```

```python
from contextlib import ExitStack

import concourse.bass as bass
from concourse import mybir

ALU = mybir.AluOpType
ACT = mybir.ActivationFunctionType
AX = mybir.AxisListType
F32 = mybir.dt.float32
F32R = mybir.dt.float32r
BF16 = mybir.dt.bfloat16
U32 = mybir.dt.uint32

P = 128
BANK = 512
HI, LO = 0, 1
PARTS = [(HI, HI), (HI, LO), (LO, HI)]

LN_EPS = 1e-5


class Signal:

    def __init__(self, sem, per_round, before=0):
        self.sem, self.per_round, self.before = sem, per_round, before

    def level(self, rnd, k):
        return rnd * self.per_round + (self.before + k)


class Room:

    def __init__(self, nc, ctx, tag):
        self.nc, self.ctx, self.tag = nc, ctx, tag

    def sb(self, name, shape, dt=F32):
        return self.ctx.enter_context(self.nc.sbuf_tensor(f"{self.tag}_{name}", shape, dt))

    def ps(self, name, shape, dt=F32):
        return self.ctx.enter_context(self.nc.psum_tensor(f"{self.tag}_{name}", shape, dt))

    def sem(self, name):
        return self.ctx.enter_context(self.nc.semaphore(f"{self.tag}_{name}"))

    def counted(self, name, per_round, before=0):
        return Signal(self.sem(name), per_round, before)


def f32(ap):
    return ap.bitcast(F32)


def cached_attention(nc, x_sb, eye, half_power, x, kv_cache, wq, wk, wv, wo):
    B, S, D = x.shape
    KV = kv_cache.shape[1]
    DC = D // P
    QT = S // P
    FULL = KV // P
    REST = KV - FULL * P
    KT = FULL + 1
    COLS = KV + S
    COLS_EVEN = COLS + COLS % 2
    TILES = KT + QT
    NB = -(-COLS // BANK)
    SCALE = float(D) ** -0.5
    assert DC == 2 and QT == 2 and FULL == 12 and NB == 4

    with ExitStack() as ctx:
        r = Room(nc, ctx, "ca")
        sb, ps, sem, counted = r.sb, r.ps, r.sem, r.counted
        w_raw = sb("w_raw", [P, 4, DC, D])
        w = sb("w", [P, 4, 2, DC, D], F32R)
        cache = sb("cache", [P, KT, D])
        stats = sb("stats", [P, QT, 6])
        mean_var = sb("mean_var", [P, QT, 2])
        fence = sb("fence", [P, 1])
        var_eps = sb("var_eps", [P, QT])
        rstd = sb("rstd", [P, QT])
        xn = sb("xn", [P, QT, D])
        xnT = sb("xnT", [P, 2, DC, S], F32R)
        qT = sb("qT", [P, 2, DC, S], F32R)
        kT = sb("kT", [P, 2, DC, COLS_EVEN], F32R)
        v = sb("v", [P, 2, TILES, D], F32R)
        probs = sb("probs", [P, QT, COLS])
        pT = sb("pT", [P, 2, TILES, S], F32R)
        oT = sb("oT", [P, 2, DC, S], F32R)
        neg_max = sb("neg_max", [P, QT])
        bias = sb("bias", [P, QT])
        row_sum = sb("row_sum", [P, QT])
        inv_sum = sb("inv_sum", [P, QT])
        ps_s = ps("ps_s", [P, NB, BANK])
        ps_t = ps("ps_t", [P, 2, BANK])
        ps_m = ps("ps_m", [P, 2, BANK])

        def to_blocks(bank, n, m=P):
            return ps_t[:, bank, 0:n * m].rearrange("p (n m) -> p n m", n=n)

        moves = [(ps_t[:, 0, :].rearrange("p (c s) -> p c s", c=DC), lambda s: xnT[:, s, :, :])]
        for c in range(DC):
            for g in range(3):
                at = 4 * g * P
                moves.append((ps_t[:, len(moves) % 2, :], lambda s, c=c, at=at: kT[:, s, c, at:at + 4 * P]))
        moves.append((to_blocks(1, DC, REST + 1)[:, :, 0:REST], lambda s: kT[:, s, :, FULL * P:KV]))
        M_CACHE = len(moves)
        moves.append((ps_m[:, 0, :].rearrange("p (c s) -> p c s", c=DC), lambda s: qT[:, s, :, :]))
        moves.append((ps_m[:, 1, :].rearrange("p (c s) -> p c s", c=DC), lambda s: kT[:, s, :, KV:COLS]))
        moves.append((ps_m[:, 0, :].rearrange("p (t d) -> p t d", t=QT), lambda s: v[:, s, KT:TILES, :]))
        M_PROBS = len(moves)
        order = [[0, 1, 2, 3], [4, 5, 6, 7], [8, 9, 10, 11], [12, 13, 14]]
        for t in range(QT):
            for k, tiles in enumerate(order):
                moves.append((to_blocks(k % 2, len(tiles)),
                              lambda s, t=t, a=tiles[0], n=len(tiles): pT[:, s, a:a + n, t * P:(t + 1) * P]))
        M_OUT = len(moves)
        moves.append((ps_m[:, 0, :].rearrange("p (c s) -> p c s", c=DC), lambda s: oT[:, s, :, :]))
        M = len(moves)

        x_in = sem("x_in")
        w_in = sem("w_in")
        cache_in = counted("cache_in", 32)
        w_turned = sem("w_turned")
        w_hi = sem("w_hi")
        w_lo = sem("w_lo")
        cleared = sem("cleared")
        ready = counted("ready", M)
        hi = counted("hi", M, before=1)
        lo = counted("lo", M, before=1)
        v_hi = counted("v_hi", 1, before=1)
        v_lo = counted("v_lo", 1, before=1)
        stat = counted("stat", 4)
        var_ready = counted("var_ready", 1)
        rstd_ready = counted("rstd_ready", 1)
        xn_ready = counted("xn_ready", 2)
        scores = counted("scores", QT)
        maxed = counted("maxed", QT)
        biased = counted("biased", QT)
        exped = counted("exped", QT, before=1)
        inverted = counted("inverted", 1)
        y_ready = counted("y_ready", 1)
        added = counted("added", QT, before=1)

        block = ctx.enter_context(nc.Block())

        @block.sync
        def _(sp):
            sp.dma_start(x_sb[:, :, :], x.rearrange("b (t p) d -> p (b t) d", p=P)).then_inc(x_in, 16)
            for n, src in enumerate((wq, wk, wv, wo)):
                sp.dma_start(w_raw[:, n, :, :], src.rearrange("(c p) d -> p c d", p=P)).then_inc(w_in, 16)
            sp.wait_ge(cleared, 3)
            with sp.Fori(0, B) as b:
                sp.wait_ge(v_lo.sem, v_lo.level(b, 0))
                sp.wait_ge(exped.sem, exped.level(b, 0))
                row = kv_cache[bass.ds(b, 1), :, :]
                sp.dma_start(cache[:, 0:FULL, :],
                             row[:, 0:FULL * P, :].rearrange("b (t p) d -> p (b t) d", p=P)
                             ).then_inc(cache_in.sem, 16)
                sp.dma_start(cache[0:REST, FULL, :], row[:, FULL * P:KV, :].rearrange("b p d -> p (b d)")
                             ).then_inc(cache_in.sem, 16)

        @block.gpsimd
        def _(pool):
            nc.gpsimd.memset(cache[:, FULL, :], 0.0).then_inc(cleared, 1)
            nc.gpsimd.memset(f32(kT[:, :, :, COLS:COLS_EVEN]), 0.0).then_inc(cleared, 1)
            nc.gpsimd.memset(f32(v[:, :, KT - 1, :]), 0.0).then_inc(cleared, 1)
            pool.wait_ge(cleared, 3)
            pool.sem_inc(v_lo.sem, 1)
            with pool.Fori(0, B) as b:
                pool.wait_ge(var_ready.sem, var_ready.level(b, 1))
                nc.gpsimd.tensor_tensor(rstd[:, :], var_eps[:, :], half_power[:, 0:QT], ALU.pow
                                        ).then_inc(rstd_ready.sem, 1)
                pool.wait_ge(v_hi.sem, v_hi.level(b, 1))
                nc.gpsimd.tensor_tensor(v[:, LO, 0:KT, :], cache[:, :, :], f32(v[:, HI, 0:KT, :]),
                                        ALU.subtract).then_inc(v_lo.sem, 1)

        @block.scalar
        def _(act):
            for n in range(4):
                act.wait_ge(w_turned, n + 1)
                nc.scalar.activation(w[:, n, HI, :, :], ps_s[:, n, :].rearrange("p (c e) -> p c e", c=DC), ACT.Copy
                                     ).then_inc(w_hi, 1)
            act.sem_inc(hi.sem, 1)
            act.sem_inc(exped.sem, 1)
            act.sem_inc(v_hi.sem, 1)
            with act.Fori(0, B) as b:
                def move_hi(m):
                    act.wait_ge(ready.sem, ready.level(b, m + 1))
                    src, dst = moves[m]
                    nc.scalar.activation(dst(HI), src, ACT.Copy).then_inc(hi.sem, 1)

                for m in range(M_CACHE):
                    move_hi(m)
                nc.scalar.activation(v[:, HI, 0:KT, :], cache[:, :, :], ACT.Copy).then_inc(v_hi.sem, 1)
                for m in range(M_CACHE, M_PROBS):
                    move_hi(m)
                for t in range(QT):
                    act.wait_ge(biased.sem, biased.level(b, t + 1))
                    nc.scalar.activation(probs[:, t, :], ps_s[:, :, :].rearrange("p n m -> p (n m)")[:, 0:COLS],
                                         ACT.Exp, bias=bias[:, t:t + 1], scale=SCALE,
                                         accum_out=row_sum[:, t:t + 1]).then_inc(exped.sem, 1)
                for m in range(M_PROBS, M):
                    move_hi(m)

        @block.vector
        def _(dve):
            dve.wait_ge(x_in, 16)
            for n in range(4):
                dve.wait_ge(w_hi, n + 1)
                nc.vector.tensor_tensor(w[:, n, LO, :, :], ps_s[:, n, :].rearrange("p (c e) -> p c e", c=DC), f32(w[:, n, HI, :, :]),
                                        ALU.subtract).then_inc(w_lo, 1)
            dve.sem_inc(lo.sem, 1)
            dve.sem_inc(added.sem, 1)
            with dve.Fori(0, B) as b:
                def move_lo(m):
                    dve.wait_ge(hi.sem, hi.level(b, m + 1))
                    src, dst = moves[m]
                    nc.vector.tensor_tensor(dst(LO), src, f32(dst(HI)), ALU.subtract).then_inc(lo.sem, 1)

                for t in range(QT):
                    nc.vector.bn_stats(stats[:, t, :], x_sb[:, bass.ds(b * QT + t, 1), :]
                                       .rearrange("p a d -> p (a d)")).then_inc(stat.sem, 1)
                dve.wait_ge(stat.sem, stat.level(b, 2))
                nc.vector.memset(fence[:, :], 0.0)
                for t in range(QT):
                    nc.vector.bn_aggr(mean_var[:, t, :], stats[:, t, :]).then_inc(stat.sem, 1)
                dve.wait_ge(stat.sem, stat.level(b, 4))
                nc.vector.tensor_scalar(var_eps[:, :], mean_var[:, :, 1], LN_EPS, None, ALU.add
                                        ).then_inc(var_ready.sem, 1)
                dve.wait_ge(rstd_ready.sem, rstd_ready.level(b, 1))
                for t in range(QT):
                    nc.vector.tensor_scalar(xn[:, t, :], x_sb[:, bass.ds(b * QT + t, 1), :]
                                            .rearrange("p a d -> p (a d)"), mean_var[:, t, 0:1],
                                            rstd[:, t:t + 1], ALU.subtract, ALU.mult).then_inc(xn_ready.sem, 1)
                for m in range(M_CACHE):
                    move_lo(m)
                for m in range(M_CACHE, M_PROBS):
                    move_lo(m)
                for t in range(QT):
                    dve.wait_ge(scores.sem, scores.level(b, t + 1))
                    nc.vector.tensor_reduce(neg_max[:, t:t + 1],
                                            ps_s[:, :, :].rearrange("p n m -> p (n m)")[:, 0:COLS],
                                            AX.X, ALU.max, negate=True).then_inc(maxed.sem, 1)
                    dve.wait_ge(maxed.sem, maxed.level(b, t + 1))
                    nc.vector.tensor_scalar(bias[:, t:t + 1], neg_max[:, t:t + 1], SCALE, None, ALU.mult
                                            ).then_inc(biased.sem, 1)
                for m in range(M_PROBS, M):
                    move_lo(m)
                nc.vector.reciprocal(inv_sum[:, :], row_sum[:, :]).then_inc(inverted.sem, 1)
                dve.wait_ge(inverted.sem, inverted.level(b, 1))
                dve.wait_ge(y_ready.sem, y_ready.level(b, 1))
                for t in range(QT):
                    row = x_sb[:, bass.ds(b * QT + t, 1), :].rearrange("p a d -> p (a d)")
                    nc.vector.scalar_tensor_tensor(row, ps_m[:, 1, t * D:(t + 1) * D], inv_sum[:, t:t + 1], row,
                                                   ALU.mult, ALU.add).then_inc(added.sem, 1)

        @block.tensor
        def _(pe):
            pe.wait_ge(w_in, 64)
            for n in range(4):
                for c in range(DC):
                    for e in range(DC):
                        mm = nc.tensor.transpose(ps_s[:, n, c * D + e * P:c * D + (e + 1) * P],
                                                 w_raw[:, n, e, c * P:(c + 1) * P], eye[:, :])
                mm.then_inc(w_turned, 1)
            pe.wait_ge(w_lo, 4)
            with pe.Fori(0, B) as b:
                def free(m):
                    pe.wait_ge(lo.sem, lo.level(b, m + 1))

                def product(out, lhs, rhs, first, last):
                    for n, (a, c) in enumerate(PARTS):
                        mm = nc.tensor.matmul(out, lhs(a), rhs(c), start=first and n == 0, stop=last and n == 2)
                    return mm

                pe.wait_ge(xn_ready.sem, xn_ready.level(b, 2))
                for c in range(DC):
                    for t in range(QT):
                        mm = nc.tensor.transpose(ps_t[:, 0, (c * QT + t) * P:(c * QT + t + 1) * P],
                                                 xn[:, t, c * P:(c + 1) * P], eye[:, :])
                mm.then_inc(ready.sem, 1)
                pe.wait_ge(cache_in.sem, cache_in.level(b, 32))
                m = 1
                for c in range(DC):
                    for g in range(3):
                        if m >= 2:
                            free(m - 2)
                        for k in range(4):
                            mm = nc.tensor.transpose(ps_t[:, m % 2, k * P:(k + 1) * P],
                                                     cache[:, 4 * g + k, c * P:(c + 1) * P], eye[:, :])
                        mm.then_inc(ready.sem, 1)
                        m += 1
                free(m - 2)
                for c in range(DC):
                    mm = nc.tensor.transpose(ps_t[:, 1, c * (REST + 1):c * (REST + 1) + REST],
                                             cache[0:REST, FULL, c * P:(c + 1) * P], eye[0:REST, 0:REST])
                mm.then_inc(ready.sem, 1)
                free(0)
                for n, bank in ((0, 0), (1, 1)):
                    for e in range(DC):
                        for c in range(DC):
                            mm = product(ps_m[:, bank, e * S:(e + 1) * S],
                                         lambda s: w[:, n, s, c, e * P:(e + 1) * P],
                                         lambda s: xnT[:, s, c, :], c == 0, c == DC - 1)
                    mm.then_inc(ready.sem, 1)
                free(M_CACHE)
                for t in range(QT):
                    for c in range(DC):
                        mm = product(ps_m[:, 0, t * D:(t + 1) * D],
                                     lambda s: xnT[:, s, c, t * P:(t + 1) * P],
                                     lambda s: w[:, 2, s, c, :], c == 0, c == DC - 1)
                mm.then_inc(ready.sem, 1)
                free(M_CACHE + 1)
                for t in range(QT):
                    pe.wait_ge(exped.sem, exped.level(b, t))
                    for n in range(NB):
                        a, z = n * BANK, min((n + 1) * BANK, COLS_EVEN)
                        for c in range(DC):
                            mm = product(ps_s[:, n, 0:z - a], lambda s: qT[:, s, c, t * P:(t + 1) * P],
                                         lambda s: kT[:, s, c, a:z], c == 0, c == DC - 1)
                    mm.then_inc(scores.sem, 1)
                m = M_PROBS
                for t in range(QT):
                    pe.wait_ge(exped.sem, exped.level(b, t + 1))
                    for k, tiles in enumerate(order):
                        free(m - 2) if m >= M_PROBS + 2 else free(M_CACHE - 1)
                        for j, tile in enumerate(tiles):
                            at = tile * P if tile < FULL else (FULL * P if tile == FULL else KV + (tile - KT) * P)
                            n = REST if tile == FULL else P
                            mm = nc.tensor.transpose(ps_t[0:n, k % 2, j * P:(j + 1) * P],
                                                     probs[:, t, at:at + n], eye[:, :])
                        mm.then_inc(ready.sem, 1)
                        m += 1
                free(M_OUT - 1)
                pe.wait_ge(v_lo.sem, v_lo.level(b, 1))
                for c in range(DC):
                    for tile in range(TILES):
                        n = REST if tile == FULL else P
                        mm = product(ps_m[:, 0, c * S:(c + 1) * S],
                                     lambda s: v[0:n, s, tile, c * P:(c + 1) * P],
                                     lambda s: pT[0:n, s, tile, :], tile == 0, tile == TILES - 1)
                mm.then_inc(ready.sem, 1)
                free(M_OUT)
                pe.wait_ge(added.sem, added.level(b, 0))
                for t in range(QT):
                    for c in range(DC):
                        mm = product(ps_m[:, 1, t * D:(t + 1) * D], lambda s: oT[:, s, c, t * P:(t + 1) * P],
                                     lambda s: w[:, 3, s, c, :], c == 0, c == DC - 1)
                mm.then_inc(y_ready.sem, 1)


def experts(nc, x_sb, eye, half_power, gate_w, wg, wu, wd, cwg, cwu, cwd):
    TT, D = x_sb.shape[1], x_sb.shape[2]
    T = TT * P
    E = gate_w.shape[0]
    I = wg.shape[2]
    CI = cwg.shape[2]
    ROUNDS = cwg.shape[0]
    U = 3
    HALVES = T // BANK
    DC = D // P
    TOP = 4
    MAX8 = 8
    SMALL_SCALE = 0.05
    assert E == 2 * ROUNDS and T == 2 * BANK and CI == P and D == 2 * P
    width = [I, I, CI]
    banks_y = TT * D // BANK

    with ExitStack() as ctx:
        r = Room(nc, ctx, "ex")
        sb, ps, sem, counted = r.sb, r.ps, r.sem, r.counted
        stats = sb("stats", [P, TT, 6])
        mean_var = sb("mean_var", [P, TT, 2])
        var_eps = sb("var_eps", [P, TT])
        rstd = sb("rstd", [P, TT])
        xn = sb("xn", [P, TT, D])
        gate = sb("gate", [E, D])
        gateT = sb("gateT", [P, 2, DC, E], F32R)
        hT = sb("hT", [P, 2, DC, T], F32R)
        logits = sb("logits", [P, TT, E])
        top = sb("top", [P, TT, MAX8])
        top_at = sb("top_at", [P, TT, MAX8], U32)
        top_index = sb("top_index", [P, TT, MAX8])
        above = sb("above", [P, TT, TOP])
        top_exp = sb("top_exp", [P, TT, TOP])
        top_sum = sb("top_sum", [P, TT])
        top_inv = sb("top_inv", [P, TT])
        weight = sb("weight", [P, TT, TOP])
        expert_id = sb("expert_id", [P, E])
        hit = sb("hit", [P, TT, E])
        part = sb("part", [P, TT, E])
        cw = sb("cw", [P, TT, E + ROUNDS])
        cw_unit = [sb(f"cw_unit{u}", [P, TT]) for u in range(U)]
        raw = [sb(f"raw{u}", [P, 2 * DC * width[u] + D]) for u in range(U)]
        w = [sb(f"w{u}", [P, 2, 2 * DC * width[u] + D], F32R) for u in range(U)]
        silu = sb("silu", [P, HALVES, BANK])
        act_gu = sb("act_gu", [P, HALVES, BANK])
        aT = [sb(f"aT{u}", [P, 2, T], F32R) for u in range(U)]
        ps_g = ps("ps_g", [P, HALVES, BANK])
        ps_u = ps("ps_u", [P, HALVES, BANK])
        ps_y = ps("ps_y", [P, banks_y, BANK])

        gate_in = sem("gate_in")
        ids = sem("ids")
        cleared = sem("cleared")
        stat = sem("stat")
        var_ready = sem("var_ready")
        rstd_ready = sem("rstd_ready")
        xn_ready = sem("xn_ready")
        turned = sem("turned")
        turned_hi = sem("turned_hi")
        turned_lo = sem("turned_lo")
        logits_ready = sem("logits_ready")
        logits_here = sem("logits_here")
        above_ready = sem("above_ready")
        exp_ready = sem("exp_ready")
        route = sem("route")
        raw_in = [counted(f"raw_in{u}", 48) for u in range(U)]
        w_hi = [counted(f"w_hi{u}", 1) for u in range(U)]
        w_lo = [counted(f"w_lo{u}", 1) for u in range(U)]
        gate_ready = counted("gate_ready", U * HALVES)
        up_ready = counted("up_ready", U * HALVES)
        silu_ready = counted("silu_ready", U * HALVES)
        a_ready = counted("a_ready", U * HALVES)
        a_hi = counted("a_hi", U * HALVES)
        a_lo = counted("a_lo", U * HALVES)
        cw_ready = counted("cw_ready", U)
        y_ready = counted("y_ready", U * banks_y)
        added = counted("added", U * TT)

        turned_moves = [(ps_y[:, c * HALVES + h, :], lambda s, c=c, h=h: hT[:, s, c, h * BANK:(h + 1) * BANK])
                        for c in range(DC) for h in range(HALVES)]
        turned_moves.append((ps_g[:, 0, 0:DC * E].rearrange("p (c e) -> p c e", c=DC),
                             lambda s: gateT[:, s, :, :]))

        block = ctx.enter_context(nc.Block())

        def rounds(eng, body):
            body(0, True, False)
            with eng.Fori(1, ROUNDS - 1) as i:
                body(i, False, False)
            body(ROUNDS - 1, False, True)

        def turn(i, u):
            return ((u - 1) % U, i + 1 if u > 0 else i)

        @block.sync
        def _(sp):
            sp.dma_start(gate[:, :], gate_w).then_inc(gate_in, 16)

            def load(i, u):
                n = width[u]
                gu = raw[u][:, 0:2 * DC * n].rearrange("p (m c i) -> p m c i", m=2, c=DC)
                for m, src in enumerate(((wg, wu), (wg, wu), (cwg, cwu))[u]):
                    e = 2 * i + u if u < 2 else i
                    sp.dma_start(gu[:, m, :, :], src[bass.ds(e, 1), :, :].rearrange("e (p c) i -> p (e c) i", p=P)
                                 ).then_inc(raw_in[u].sem, 16)
                src = (wd, wd, cwd)[u]
                sp.dma_start(raw[u][0:n, 2 * DC * n:2 * DC * n + D],
                             src[bass.ds(e, 1), :, :].rearrange("e i d -> (e i) d")).then_inc(raw_in[u].sem, 16)

            sp.wait_ge(cleared, 2)
            for u in range(U):
                load(0, u)

            def ahead(i):
                for u in range(U):
                    sp.wait_ge(w_lo[u].sem, w_lo[u].level(i, 0))
                    load(i, u)

            with sp.Fori(1, ROUNDS) as i:
                ahead(i)

        @block.gpsimd
        def _(pool):
            nc.gpsimd.iota(expert_id[:, :], [[1, E]], base=0, channel_multiplier=0,
                           allow_small_or_imprecise_dtypes=True).then_inc(ids, 1)
            for u in range(2):
                nc.gpsimd.memset(raw[u][:, 2 * DC * I:2 * DC * I + D], 0.0).then_inc(cleared, 1)
            pool.wait_ge(var_ready, 1)
            nc.gpsimd.tensor_tensor(rstd[:, :], var_eps[:, :], half_power[:, 0:TT], ALU.pow).then_inc(rstd_ready, 1)

            def w_low(i, u):
                pool.wait_ge(w_hi[u].sem, w_hi[u].level(i, 1))
                nc.gpsimd.tensor_tensor(w[u][:, LO, :], raw[u][:, :], f32(w[u][:, HI, :]), ALU.subtract
                                        ).then_inc(w_lo[u].sem, 1)

            w_low(0, 0)
            w_low(0, 1)

            def body(i, first, last):
                for u in range(U):
                    n = width[u]
                    for h in range(HALVES):
                        pool.wait_ge(a_hi.sem, a_hi.level(i, u * HALVES + h + 1))
                        nc.gpsimd.tensor_tensor(aT[u][0:n, LO, h * BANK:(h + 1) * BANK], act_gu[0:n, h, :],
                                                f32(aT[u][0:n, HI, h * BANK:(h + 1) * BANK]), ALU.subtract
                                                ).then_inc(a_lo.sem, 1)
                    slot, at = turn(i, u)
                    if not (last and u > 0):
                        w_low(at, slot)

            rounds(pool, body)

        @block.scalar
        def _(act):
            for m in range(HALVES * DC + 1):
                act.wait_ge(turned, m + 1)
                src, dst = turned_moves[m]
                nc.scalar.activation(dst(HI), src, ACT.Copy).then_inc(turned_hi, 1)
            act.wait_ge(above_ready, 1)
            nc.scalar.activation(top_exp[:, :, :], above[:, :, :], ACT.Exp).then_inc(exp_ready, 1)

            def w_high(i, u, waits):
                if waits:
                    act.wait_ge(y_ready.sem, y_ready.level(i, (u + 1) * banks_y - U * banks_y))
                act.wait_ge(raw_in[u].sem, raw_in[u].level(i, 48))
                nc.scalar.activation(w[u][:, HI, :], raw[u][:, :], ACT.Copy).then_inc(w_hi[u].sem, 1)

            w_high(0, 0, False)
            w_high(0, 1, False)

            def body(i, first, last):
                for u in range(U):
                    n = width[u]
                    for h in range(HALVES):
                        act.wait_ge(gate_ready.sem, gate_ready.level(i, u * HALVES + h + 1))
                        if not (first and u == 0):
                            act.wait_ge(a_ready.sem, a_ready.level(i, (u - 1) * HALVES + h + 1))
                        nc.scalar.activation(silu[0:n, h, :], ps_g[0:n, h, :], ACT.Silu).then_inc(silu_ready.sem, 1)
                    for h in range(HALVES):
                        if h == 0 and not first:
                            act.wait_ge(y_ready.sem, y_ready.level(i, (u + 1) * banks_y - U * banks_y))
                        act.wait_ge(a_ready.sem, a_ready.level(i, u * HALVES + h + 1))
                        nc.scalar.activation(aT[u][0:n, HI, h * BANK:(h + 1) * BANK], act_gu[0:n, h, :], ACT.Copy
                                             ).then_inc(a_hi.sem, 1)
                    slot, at = turn(i, u)
                    if not (last and u > 0):
                        w_high(at, slot, not (first and u == 0))

            rounds(act, body)

        @block.vector
        def _(dve):
            for t in range(TT):
                nc.vector.bn_stats(stats[:, t, :], x_sb[:, t, :]).then_inc(stat, 1)
            dve.wait_ge(stat, TT)
            for t in range(TT):
                nc.vector.bn_aggr(mean_var[:, t, :], stats[:, t, :]).then_inc(stat, 1)
            dve.wait_ge(stat, 2 * TT)
            nc.vector.tensor_scalar(var_eps[:, :], mean_var[:, :, 1], LN_EPS, None, ALU.add).then_inc(var_ready, 1)
            dve.wait_ge(rstd_ready, 1)
            for t in range(TT):
                nc.vector.tensor_scalar(xn[:, t, :], x_sb[:, t, :], mean_var[:, t, 0:1], rstd[:, t:t + 1],
                                        ALU.subtract, ALU.mult).then_inc(xn_ready, 1)
            for m in range(HALVES * DC + 1):
                dve.wait_ge(turned_hi, m + 1)
                src, dst = turned_moves[m]
                nc.vector.tensor_tensor(dst(LO), src, f32(dst(HI)), ALU.subtract).then_inc(turned_lo, 1)
            dve.wait_ge(logits_ready, 1)
            nc.vector.tensor_copy(logits[:, :, :], ps_y[:, 0, 0:TT * E].rearrange("p (t e) -> p t e", t=TT)
                                  ).then_inc(logits_here, 1)
            dve.wait_ge(logits_here, 1)
            step = [0]

            def then(ins):
                step[0] += 1
                ins.then_inc(route, 1)
                dve.wait_ge(route, step[0])

            for t in range(TT):
                then(nc.vector.max(top[:, t, :], logits[:, t, :]))
                then(nc.vector.max_index(top_at[:, t, :], top[:, t, :], logits[:, t, :]))
            then(nc.vector.tensor_copy(top_index[:, :, :], top_at[:, :, :]))
            nc.vector.tensor_tensor(above[:, :, :], top[:, :, 0:TOP], top[:, :, 0:1].broadcast_to([P, TT, TOP]),
                                    ALU.subtract).then_inc(above_ready, 1)
            dve.wait_ge(exp_ready, 1)
            then(nc.vector.tensor_reduce(top_sum[:, :], top_exp[:, :, :], AX.X, ALU.add))
            then(nc.vector.reciprocal(top_inv[:, :], top_sum[:, :]))
            then(nc.vector.tensor_tensor(weight[:, :, :], top_exp[:, :, :],
                                         top_inv[:, :].unsqueeze(2).broadcast_to([P, TT, TOP]), ALU.mult))
            dve.wait_ge(ids, 1)
            for k in range(TOP):
                then(nc.vector.tensor_tensor(hit[:, :, :], expert_id[:, :].unsqueeze(1).broadcast_to([P, TT, E]),
                                             top_index[:, :, k:k + 1].broadcast_to([P, TT, E]), ALU.is_equal))
                dst = cw[:, :, 0:E] if k == 0 else part[:, :, :]
                then(nc.vector.tensor_tensor(dst, hit[:, :, :], weight[:, :, k:k + 1].broadcast_to([P, TT, E]),
                                             ALU.mult))
                if k:
                    then(nc.vector.tensor_tensor(cw[:, :, 0:E], cw[:, :, 0:E], part[:, :, :], ALU.add))
            pairs = cw[:, :, 0:E].rearrange("p t (c g) -> p t c g", g=2)
            then(nc.vector.tensor_tensor(part[:, :, 0:ROUNDS], pairs[:, :, :, 0], pairs[:, :, :, 1], ALU.add))
            then(nc.vector.tensor_scalar(cw[:, :, E:E + ROUNDS], part[:, :, 0:ROUNDS], SMALL_SCALE, None, ALU.mult))

            def add(i, u):
                for t in range(TT):
                    dve.wait_ge(y_ready.sem, y_ready.level(i, u * banks_y + t // 2 + 1))
                    if t == 0:
                        dve.wait_ge(cw_ready.sem, cw_ready.level(i, u + 1))
                    nc.vector.scalar_tensor_tensor(x_sb[:, t, :], ps_y[:, t // 2, (t % 2) * D:(t % 2 + 1) * D],
                                                   cw_unit[u][:, t:t + 1], x_sb[:, t, :], ALU.mult, ALU.add
                                                   ).then_inc(added.sem, 1)

            def body(i, first, last):
                for u in range(U):
                    n = width[u]
                    e = 2 * i + u if u < 2 else E + i
                    nc.vector.tensor_copy(cw_unit[u][:, :].unsqueeze(2), cw[:, :, bass.ds(e, 1)]
                                          ).then_inc(cw_ready.sem, 1)
                    for h in range(HALVES):
                        if not (first and u == 0):
                            dve.wait_ge(a_lo.sem, a_lo.level(i, (u - 1) * HALVES + h + 1))
                        dve.wait_ge(silu_ready.sem, silu_ready.level(i, u * HALVES + h + 1))
                        dve.wait_ge(up_ready.sem, up_ready.level(i, u * HALVES + h + 1))
                        nc.vector.tensor_tensor(act_gu[0:n, h, :], silu[0:n, h, :], ps_u[0:n, h, :], ALU.mult
                                                ).then_inc(a_ready.sem, 1)
                    if u > 0:
                        add(i, u - 1)
                    elif not first:
                        add(i - 1, U - 1)

            rounds(dve, body)
            add(ROUNDS - 1, U - 1)

        @block.tensor
        def _(pe):
            def product(out, lhs, rhs, first, last):
                for n, (a, c) in enumerate(PARTS):
                    mm = nc.tensor.matmul(out, lhs(a), rhs(c), start=first and n == 0, stop=last and n == 2)
                return mm

            pe.wait_ge(xn_ready, TT)
            for c in range(DC):
                for h in range(HALVES):
                    for k in range(4):
                        mm = nc.tensor.transpose(ps_y[:, c * HALVES + h, k * P:(k + 1) * P],
                                                 xn[:, 4 * h + k, :].rearrange("p (q c) -> p q c", c=DC)[:, :, c],
                                                 eye[:, :])
                    mm.then_inc(turned, 1)
            pe.wait_ge(gate_in, 16)
            for c in range(DC):
                mm = nc.tensor.transpose(ps_g[:, 0, c * E:(c + 1) * E],
                                         gate[:, :].rearrange("e (q c) -> e q c", c=DC)[:, :, c], eye[0:E, 0:E])
            mm.then_inc(turned, 1)
            pe.wait_ge(turned_lo, HALVES * DC + 1)
            for t in range(TT):
                for c in range(DC):
                    mm = product(ps_y[:, 0, t * E:(t + 1) * E], lambda s: hT[:, s, c, t * P:(t + 1) * P],
                                 lambda s: gateT[:, s, c, :], c == 0, c == DC - 1)
            mm.then_inc(logits_ready, 1)
            pe.wait_ge(logits_here, 1)

            def gate_up(i, u, first):
                n = width[u]
                pe.wait_ge(w_lo[u].sem, w_lo[u].level(i, 1))
                for h in range(HALVES):
                    if not first:
                        pe.wait_ge(a_ready.sem, a_ready.level(i, (u - 1) * HALVES + h + 1))
                    for m, (bank, done) in enumerate(((ps_g, gate_ready), (ps_u, up_ready))):
                        for c in range(DC):
                            mm = product(bank[0:n, h, :], lambda s: w[u][:, s, (m * DC + c) * n:(m * DC + c + 1) * n],
                                         lambda s: hT[:, s, c, h * BANK:(h + 1) * BANK], c == 0, c == DC - 1)
                        mm.then_inc(done.sem, 1)

            def down(i, u, first):
                n = width[u]
                for t in range(TT):
                    if t % 4 == 0:
                        pe.wait_ge(a_lo.sem, a_lo.level(i, u * HALVES + t // 4 + 1))
                    if not first and t % 2 == 0:
                        pe.wait_ge(added.sem, added.level(i, (u - 1) * TT + t + 2))
                    mm = product(ps_y[:, t // 2, (t % 2) * D:(t % 2 + 1) * D],
                                 lambda s: aT[u][0:n, s, t * P:(t + 1) * P],
                                 lambda s: w[u][0:n, s, 2 * DC * n:2 * DC * n + D], True, True)
                    if t % 2 == 1:
                        mm.then_inc(y_ready.sem, 1)

            def body(i, first, last):
                for u in range(U):
                    gate_up(i, u, first and u == 0)
                    if u > 0:
                        down(i, u - 1, first and u == 1)
                    elif not first:
                        down(i - 1, U - 1, False)

            rounds(pe, body)
            down(ROUNDS - 1, U - 1, False)


def grouped_attention(nc, x_sb, eye, half_power, encoder, wq, wk, wv, wo, q_norm_w, k_norm_w):
    TT, D = x_sb.shape[1], x_sb.shape[2]
    B, KV, _ = encoder.shape
    QT = TT // B
    S = QT * P
    DH = q_norm_w.shape[0]
    G = wk.shape[1] // DH
    HG = wq.shape[1] // (G * DH)
    DC = D // P
    FULL = KV // P
    REST = KV - FULL * P
    KT = FULL + 1
    COLS_EVEN = KV + KV % 2
    NB = -(-KV // BANK)
    RMS_EPS = 1e-6
    STEPS = HG * QT
    KVJ = (KT + 1) // 2
    WQ, WKV, WO = DC * HG * DH, DC * 2 * DH, HG * D
    assert DH == P and DC == 2 and QT == 2 and HG == 4 and NB == 4 and FULL == 12
    HALF = 2 * BANK

    with ExitStack() as ctx:
        r = Room(nc, ctx, "ga")
        sb, ps, sem, counted = r.sb, r.ps, r.sem, r.counted
        w_in_raw = sb("w_in_raw", [P, WQ + WKV])
        w_in = sb("w_in", [P, 2, WQ + WKV], F32R)
        w_out_raw = sb("w_out_raw", [P, WO])
        w_out = sb("w_out", [P, 2, WO], F32R)
        norm_w = sb("norm_w", [P, 2])
        qk_w = sb("qk_w", [P, 1])
        fence = sb("fence", [P, 1])
        enc = sb("enc", [P, KT, D])
        encT = sb("encT", [P, 2, DC, COLS_EVEN], F32R)
        stats = sb("stats", [P, QT, 6])
        mean_var = sb("mean_var", [P, QT, 2])
        var_eps = sb("var_eps", [P, QT])
        rstd = sb("rstd", [P, QT])
        xn = sb("xn", [P, QT, D])
        hT = sb("hT", [P, 2, DC, S], F32R)
        q_sq = sb("q_sq", [P, QT * HG])
        q_sq_eps = sb("q_sq_eps", [P, QT * HG])
        q_scale = sb("q_scale", [P, QT * HG])
        k_sq = sb("k_sq", [P, KT])
        k_sq_eps = sb("k_sq_eps", [P, KT])
        k_scale = sb("k_scale", [P, KT])
        qn = sb("qn", [P, QT, HG * DH])
        k_raw = sb("k_raw", [P, KT, DH])
        kn = sb("kn", [P, KT, DH])
        qT = sb("qT", [P, 2, HG, S], F32R)
        kT = sb("kT", [P, 2, COLS_EVEN], F32R)
        v = sb("v", [P, 2, KT, DH], F32R)
        probs = [sb(f"probs{i}", [P, KV]) for i in range(2)]
        bank_max = sb("bank_max", [P, NB])
        neg_max = sb("neg_max", [P, 2])
        half_sum = sb("half_sum", [P, 2, 2])
        row_sum = sb("row_sum", [P, 1])
        inv_sum = sb("inv_sum", [P, 1])
        pT = [sb(f"pT{i}", [P, 2, KT, S], F32R) for i in range(2)]
        oT = sb("oT", [P, 2, HG, S], F32R)
        ps_s = ps("ps_s", [P, NB, BANK])
        ps_t = ps("ps_t", [P, 2, BANK])
        ps_m = ps("ps_m", [P, 2, BANK])

        row_moves = [(ps_t[:, 0, :].rearrange("p (c s) -> p c s", c=DC), lambda s: hT[:, s, :, :])]
        for c in range(DC):
            for g in range(3):
                at = 4 * g * P
                row_moves.append((ps_t[:, len(row_moves) % 2, :],
                                  lambda s, c=c, at=at: encT[:, s, c, at:at + 4 * P]))
        row_moves.append((ps_t[:, 1, 0:DC * (REST + 1)].rearrange("p (c n) -> p c n", c=DC)[:, :, 0:REST],
                          lambda s: encT[:, s, :, FULL * P:KV]))
        RM = len(row_moves)
        key_tiles = [range(0, 4), range(4, 8), range(8, 12), range(12, 13)]
        moves = []
        for t in range(QT):
            moves.append((ps_t[:, t, :].rearrange("p (h s) -> p h s", h=HG),
                          lambda s, t=t: qT[:, s, :, t * P:(t + 1) * P]))
        M_KEYS = len(moves)
        for tiles in key_tiles:
            n = P * len(tiles) if tiles[0] < FULL else REST
            moves.append((ps_t[:, len(moves) % 2, 0:n], lambda s, a=tiles[0] * P, n=n: kT[:, s, a:a + n]))
        M_PROBS = len(moves)
        for n in range(STEPS):
            h, t = n // QT, n % QT
            for tiles in key_tiles:
                a, k = tiles[0], len(tiles)
                rows = P if a < FULL else REST
                moves.append((ps_t[0:rows, len(moves) % 2, 0:k * P].rearrange("p (k s) -> p k s", k=k),
                              lambda s, a=a, k=k, h=h, t=t, rows=rows:
                              pT[h % 2][0:rows, s, a:a + k, t * P:(t + 1) * P]))
        M = len(moves)
        JOBS = len(key_tiles)

        cleared = sem("cleared")
        norm_in = sem("norm_in")
        qk_ready = sem("qk_ready")
        ones_ready = sem("ones_ready")
        w_in_in = counted("w_in_in", 48)
        w_out_in = counted("w_out_in", 16)
        w_in_hi = counted("w_in_hi", 1)
        w_in_lo = counted("w_in_lo", 1, before=1)
        w_out_hi = counted("w_out_hi", 1)
        w_out_lo = counted("w_out_lo", 1, before=1)
        enc_in = counted("enc_in", 32)
        stat = counted("stat", 4)
        var_ready = counted("var_ready", 1)
        rstd_ready = counted("rstd_ready", 1)
        xn_ready = counted("xn_ready", 1)
        row_ready = counted("row_ready", RM)
        row_hi = counted("row_hi", RM)
        row_lo = counted("row_lo", RM, before=1)
        q_ready = counted("q_ready", QT)
        q_squared = counted("q_squared", 1)
        q_eps = counted("q_eps", 1)
        q_scaled = counted("q_scaled", 1)
        q_normed = counted("q_normed", QT)
        kv_ready = counted("kv_ready", KVJ)
        kv_squared = counted("kv_squared", KVJ)
        kv_moved = counted("kv_moved", KVJ)
        k_eps = counted("k_eps", 1)
        k_scaled = counted("k_scaled", 1)
        k_normed = counted("k_normed", 1)
        turned = counted("turned", M)
        hi = counted("hi", M)
        lo = counted("lo", M, before=1)
        scores = counted("scores", STEPS * NB)
        maxed = counted("maxed", STEPS)
        neg_ready = counted("neg_ready", STEPS)
        exped = counted("exped", 2 * STEPS, before=1)
        summed = counted("summed", STEPS)
        inverted = counted("inverted", STEPS)
        normed = counted("normed", STEPS)
        o_ready = counted("o_ready", HG)
        o_hi = counted("o_hi", HG)
        o_lo = counted("o_lo", HG)
        y_ready = counted("y_ready", 1, before=1)
        added = counted("added", 1, before=1)

        block = ctx.enter_context(nc.Block())

        def rounds(eng, row, body):
            with eng.Fori(0, B) as b:
                row(b)
                with eng.Fori(0, G) as g:
                    body(b, b * G + g)

        @block.sync
        def _(sp):
            sp.dma_start(norm_w[:, 0:1], q_norm_w.rearrange("(p a) -> p a", a=1)).then_inc(norm_in, 16)
            sp.dma_start(norm_w[:, 1:2], k_norm_w.rearrange("(p a) -> p a", a=1)).then_inc(norm_in, 16)
            sp.wait_ge(cleared, 4)

            def load_weights(g, n):
                sp.wait_ge(w_in_lo.sem, w_in_lo.level(n, 0))
                sp.dma_start(w_in_raw[:, 0:WQ].rearrange("p (c e) -> p c e", c=DC),
                             wq.rearrange("(c p) e -> p c e", p=P)[:, :, bass.ds(g * (HG * DH), HG * DH)]
                             ).then_inc(w_in_in.sem, 16)
                kv = w_in_raw[:, WQ:WQ + WKV].rearrange("p (c m e) -> p c m e", c=DC, m=2)
                for m, src in enumerate((wk, wv)):
                    sp.dma_start(kv[:, :, m, :], src.rearrange("(c p) e -> p c e", p=P)[:, :, bass.ds(g * DH, DH)]
                                 ).then_inc(w_in_in.sem, 16)
                sp.wait_ge(w_out_lo.sem, w_out_lo.level(n, 0))
                sp.dma_start(w_out_raw[:, :].rearrange("p (h d) -> p h d", h=HG),
                             wo[bass.ds(g * (HG * DH), HG * DH), :].rearrange("(h p) d -> p h d", p=P)
                             ).then_inc(w_out_in.sem, 16)

            with sp.Fori(0, B) as b:
                sp.wait_ge(row_lo.sem, row_lo.level(b, 0))
                row = encoder[bass.ds(b, 1), :, :]
                sp.dma_start(enc[:, 0:FULL, :], row[:, 0:FULL * P, :].rearrange("b (t p) d -> p (b t) d", p=P)
                             ).then_inc(enc_in.sem, 16)
                sp.dma_start(enc[0:REST, FULL, :], row[:, FULL * P:KV, :].rearrange("b p d -> p (b d)")
                             ).then_inc(enc_in.sem, 16)
                with sp.Fori(0, G) as g:
                    load_weights(g, b * G + g)
            load_weights(0, B * G)
            sp.wait_ge(w_in_in.sem, w_in_in.level(B * G, 48))
            sp.wait_ge(w_out_in.sem, w_out_in.level(B * G, 16))

        @block.gpsimd
        def _(pool):
            nc.gpsimd.memset(k_raw[:, FULL, :], 0.0).then_inc(cleared, 1)
            nc.gpsimd.memset(k_sq[:, FULL:KT], 1.0).then_inc(cleared, 1)
            nc.gpsimd.memset(f32(kT[:, :, KV:COLS_EVEN]), 0.0).then_inc(cleared, 1)
            nc.gpsimd.memset(f32(v[:, :, FULL, :]), 0.0).then_inc(cleared, 1)
            pool.sem_inc(w_in_lo.sem, 1)
            pool.sem_inc(w_out_lo.sem, 1)

            def split_in(n):
                pool.wait_ge(w_in_hi.sem, w_in_hi.level(n, 1))
                nc.gpsimd.tensor_tensor(w_in[:, LO, :], w_in_raw[:, :], f32(w_in[:, HI, :]), ALU.subtract
                                        ).then_inc(w_in_lo.sem, 1)

            def split_out(n):
                pool.wait_ge(w_out_hi.sem, w_out_hi.level(n, 1))
                nc.gpsimd.tensor_tensor(w_out[:, LO, :], w_out_raw[:, :], f32(w_out[:, HI, :]), ALU.subtract
                                        ).then_inc(w_out_lo.sem, 1)

            split_in(0)

            def row(b):
                pool.wait_ge(var_ready.sem, var_ready.level(b, 1))
                nc.gpsimd.tensor_tensor(rstd[:, :], var_eps[:, :], half_power[:, 0:QT], ALU.pow
                                        ).then_inc(rstd_ready.sem, 1)

            def body(b, n):
                pool.wait_ge(q_eps.sem, q_eps.level(n, 1))
                nc.gpsimd.tensor_tensor(q_scale[:, :], q_sq_eps[:, :], half_power[:, 0:QT * HG], ALU.pow
                                        ).then_inc(q_scaled.sem, 1)
                pool.wait_ge(k_eps.sem, k_eps.level(n, 1))
                nc.gpsimd.tensor_tensor(k_scale[:, :], k_sq_eps[:, :], half_power[:, 0:KT], ALU.pow
                                        ).then_inc(k_scaled.sem, 1)
                split_out(n)
                split_in(n + 1)

            rounds(pool, row, body)

        @block.scalar
        def _(act):
            act.sem_inc(exped.sem, 1)

            def split_in(n):
                act.wait_ge(w_in_in.sem, w_in_in.level(n, 48))
                nc.scalar.activation(w_in[:, HI, :], w_in_raw[:, :], ACT.Copy).then_inc(w_in_hi.sem, 1)

            split_in(0)

            def row(b):
                for m, (src, dst) in enumerate(row_moves):
                    act.wait_ge(row_ready.sem, row_ready.level(b, m + 1))
                    nc.scalar.activation(dst(HI), src, ACT.Copy).then_inc(row_hi.sem, 1)

            def body(b, n):
                def move_hi(m, scale=1.0):
                    act.wait_ge(turned.sem, turned.level(n, m + 1))
                    src, dst = moves[m]
                    nc.scalar.activation(dst(HI), src, ACT.Copy, scale=scale).then_inc(hi.sem, 1)

                for t in range(QT):
                    act.wait_ge(q_ready.sem, q_ready.level(n, t + 1))
                    for h in range(HG):
                        k = t * HG + h
                        last = nc.scalar.activation(qn[:, t, h * DH:(h + 1) * DH], ps_m[:, t, h * DH:(h + 1) * DH], ACT.Square,
                                                    accum_out=q_sq[:, k:k + 1])
                last.then_inc(q_squared.sem, 1)
                for j in range(KVJ):
                    act.wait_ge(kv_ready.sem, kv_ready.level(n, j + 1))
                    tiles = range(2 * j, min(2 * j + 2, KT))
                    rows = P if tiles[-1] < FULL else REST
                    bank = ps_s[0:rows, j % NB, 0:len(tiles) * 2 * DH].rearrange("p (t m d) -> p t m d", m=2, d=DH)
                    for i, tile in enumerate(tiles):
                        nc.scalar.activation(kn[0:rows, tile, :], bank[:, i, 0, :], ACT.Square,
                                             accum_out=k_sq[0:rows, tile:tile + 1])
                    nc.scalar.activation(v[0:rows, HI, tiles[0]:tiles[-1] + 1, :], bank[:, :, 1, :], ACT.Copy
                                         ).then_inc(kv_squared.sem, 1)
                for m in range(M_KEYS):
                    move_hi(m)
                act.wait_ge(qk_ready, 1)
                for m in range(M_KEYS, M_PROBS):
                    move_hi(m, qk_w[:, 0:1])

                def exp(step):
                    act.wait_ge(neg_ready.sem, neg_ready.level(n, step + 1))
                    for k, (a, z) in enumerate(((0, HALF), (HALF, KV))):
                        nc.scalar.activation(probs[step % 2][:, a:z],
                                             ps_s[:, :, :].rearrange("p n m -> p (n m)")[:, a:z], ACT.Exp,
                                             bias=neg_max[:, step % 2:step % 2 + 1],
                                             accum_out=half_sum[:, step % 2, k:k + 1]).then_inc(exped.sem, 1)

                def out_hi(h):
                    act.wait_ge(o_ready.sem, o_ready.level(n, h + 1))
                    nc.scalar.activation(oT[:, HI, h, :], ps_m[:, h % 2, 0:S], ACT.Copy).then_inc(o_hi.sem, 1)

                for step in range(STEPS + 1):
                    m = M_PROBS + (step - 1) * JOBS
                    if step > 0:
                        move_hi(m)
                        move_hi(m + 1)
                    if step < STEPS:
                        exp(step)
                    if step > 0:
                        move_hi(m + 2)
                        move_hi(m + 3)
                    if step >= 5 and step % 2 == 1:
                        out_hi((step - 5) // 2)
                    if step == 2:
                        act.wait_ge(w_out_in.sem, w_out_in.level(n, 16))
                        act.wait_ge(y_ready.sem, y_ready.level(n, 0))
                        nc.scalar.activation(w_out[:, HI, :], w_out_raw[:, :], ACT.Copy).then_inc(w_out_hi.sem, 1)
                    if step == 4:
                        split_in(n + 1)
                for h in range(HG - 2, HG):
                    out_hi(h)

            rounds(act, row, body)

        @block.vector
        def _(dve):
            dve.wait_ge(norm_in, 32)
            nc.vector.tensor_tensor(qk_w[:, :], norm_w[:, 0:1], norm_w[:, 1:2], ALU.mult).then_inc(qk_ready, 1)
            dve.sem_inc(row_lo.sem, 1)
            dve.sem_inc(lo.sem, 1)
            dve.sem_inc(added.sem, 1)

            def row(b):
                for t in range(QT):
                    nc.vector.bn_stats(stats[:, t, :], x_sb[:, bass.ds(b * QT + t, 1), :]
                                       .rearrange("p a d -> p (a d)")).then_inc(stat.sem, 1)
                dve.wait_ge(stat.sem, stat.level(b, QT))
                nc.vector.memset(fence[:, :], 0.0)
                for t in range(QT):
                    nc.vector.bn_aggr(mean_var[:, t, :], stats[:, t, :]).then_inc(stat.sem, 1)
                dve.wait_ge(stat.sem, stat.level(b, 2 * QT))
                nc.vector.tensor_scalar(var_eps[:, :], mean_var[:, :, 1], LN_EPS, None, ALU.add
                                        ).then_inc(var_ready.sem, 1)
                dve.wait_ge(rstd_ready.sem, rstd_ready.level(b, 1))
                for t in range(QT):
                    last = nc.vector.tensor_scalar(xn[:, t, :], x_sb[:, bass.ds(b * QT + t, 1), :]
                                                   .rearrange("p a d -> p (a d)"), mean_var[:, t, 0:1],
                                                   rstd[:, t:t + 1], ALU.subtract, ALU.mult)
                last.then_inc(xn_ready.sem, 1)
                for m, (src, dst) in enumerate(row_moves):
                    dve.wait_ge(row_hi.sem, row_hi.level(b, m + 1))
                    nc.vector.tensor_tensor(dst(LO), src, f32(dst(HI)), ALU.subtract).then_inc(row_lo.sem, 1)

            def body(b, n):
                def move_lo(m):
                    dve.wait_ge(hi.sem, hi.level(n, m + 1))
                    src, dst = moves[m]
                    if M_KEYS <= m < M_PROBS:
                        ins = nc.vector.scalar_tensor_tensor(dst(LO), src, qk_w[:, 0:1], f32(dst(HI)),
                                                             ALU.mult, ALU.subtract)
                    else:
                        ins = nc.vector.tensor_tensor(dst(LO), src, f32(dst(HI)), ALU.subtract)
                    ins.then_inc(lo.sem, 1)

                dve.wait_ge(q_squared.sem, q_squared.level(n, 1))
                nc.vector.tensor_scalar(q_sq_eps[:, :], q_sq[:, :], DH * RMS_EPS, None, ALU.add
                                        ).then_inc(q_eps.sem, 1)
                dve.wait_ge(q_scaled.sem, q_scaled.level(n, 1))
                for t in range(QT):
                    nc.vector.tensor_tensor(
                        qn[:, t, :].rearrange("p (h d) -> p h d", h=HG),
                        ps_m[:, t, :].rearrange("p (h d) -> p h d", h=HG),
                        q_scale[:, t * HG:(t + 1) * HG].unsqueeze(2).broadcast_to([P, HG, DH]), ALU.mult
                    ).then_inc(q_normed.sem, 1)
                for j in range(KVJ):
                    dve.wait_ge(kv_squared.sem, kv_squared.level(n, j + 1))
                    tiles = range(2 * j, min(2 * j + 2, KT))
                    rows = P if tiles[-1] < FULL else REST
                    bank = ps_s[0:rows, j % NB, 0:len(tiles) * 2 * DH].rearrange("p (t m d) -> p t m d", m=2, d=DH)
                    at = slice(tiles[0], tiles[-1] + 1)
                    nc.vector.tensor_copy(k_raw[0:rows, at, :], bank[:, :, 0, :])
                    nc.vector.tensor_tensor(v[0:rows, LO, at, :], bank[:, :, 1, :], f32(v[0:rows, HI, at, :]),
                                            ALU.subtract).then_inc(kv_moved.sem, 1)
                nc.vector.tensor_scalar(k_sq_eps[:, :], k_sq[:, :], 1.0 / DH, RMS_EPS, ALU.mult, ALU.add
                                        ).then_inc(k_eps.sem, 1)
                for m in range(M_KEYS):
                    move_lo(m)
                dve.wait_ge(kv_moved.sem, kv_moved.level(n, KVJ))
                dve.wait_ge(k_scaled.sem, k_scaled.level(n, 1))
                nc.vector.tensor_tensor(kn[:, :, :], k_raw[:, :, :],
                                        k_scale[:, :].unsqueeze(2).broadcast_to([P, KT, DH]), ALU.mult
                                        ).then_inc(k_normed.sem, 1)
                for m in range(M_KEYS, M_PROBS):
                    move_lo(m)

                def largest(step):
                    for k in range(NB):
                        dve.wait_ge(scores.sem, scores.level(n, step * NB + k + 1))
                        last = nc.vector.tensor_reduce(bank_max[:, k:k + 1], ps_s[:, k, 0:min(BANK, KV - k * BANK)],
                                                       AX.X, ALU.max)
                    last.then_inc(maxed.sem, 1)
                    dve.wait_ge(maxed.sem, maxed.level(n, step + 1))
                    nc.vector.tensor_reduce(neg_max[:, step % 2:step % 2 + 1], bank_max[:, :], AX.X, ALU.max,
                                            negate=True).then_inc(neg_ready.sem, 1)

                def normalize(step):
                    dve.wait_ge(exped.sem, exped.level(n, 2 * step + 2))
                    nc.vector.tensor_tensor(row_sum[:, :], half_sum[:, step % 2, 0:1], half_sum[:, step % 2, 1:2],
                                            ALU.add).then_inc(summed.sem, 1)
                    dve.wait_ge(summed.sem, summed.level(n, step + 1))
                    nc.vector.reciprocal(inv_sum[:, :], row_sum[:, :]).then_inc(inverted.sem, 1)
                    dve.wait_ge(inverted.sem, inverted.level(n, step + 1))
                    p = probs[step % 2]
                    nc.vector.tensor_scalar(p[:, :], p[:, :], inv_sum[:, 0:1], None, ALU.mult
                                            ).then_inc(normed.sem, 1)

                def out_lo(h):
                    dve.wait_ge(o_hi.sem, o_hi.level(n, h + 1))
                    nc.vector.tensor_tensor(oT[:, LO, h, :], ps_m[:, h % 2, 0:S], f32(oT[:, HI, h, :]),
                                            ALU.subtract).then_inc(o_lo.sem, 1)

                for step in range(STEPS + 1):
                    if step > 0:
                        normalize(step - 1)
                    if step < STEPS:
                        largest(step)
                    if step > 0:
                        for k in range(JOBS):
                            move_lo(M_PROBS + (step - 1) * JOBS + k)
                    if step >= 5 and step % 2 == 1:
                        out_lo((step - 5) // 2)
                for h in range(HG - 2, HG):
                    out_lo(h)
                dve.wait_ge(y_ready.sem, y_ready.level(n, 1))
                rows = x_sb[:, bass.ds(b * QT, QT), :]
                nc.vector.tensor_tensor(rows, rows, ps_m[:, 0, :].rearrange("p (t d) -> p t d", t=QT), ALU.add
                                        ).then_inc(added.sem, 1)

            rounds(dve, row, body)

        @block.tensor
        def _(pe):
            def product(out, lhs, rhs, first, last):
                for n, (a, c) in enumerate(PARTS):
                    mm = nc.tensor.matmul(out, lhs(a), rhs(c), start=first and n == 0, stop=last and n == 2)
                return mm

            pe.sem_inc(y_ready.sem, 1)
            pe.wait_ge(cleared, 4)

            def row(b):
                def free(m):
                    pe.wait_ge(row_lo.sem, row_lo.level(b, m + 1))

                pe.wait_ge(lo.sem, lo.level(b * G, 0))
                pe.wait_ge(xn_ready.sem, xn_ready.level(b, 1))
                for c in range(DC):
                    for t in range(QT):
                        mm = nc.tensor.transpose(ps_t[:, 0, (c * QT + t) * P:(c * QT + t + 1) * P],
                                                 xn[:, t, c * P:(c + 1) * P], eye[:, :])
                mm.then_inc(row_ready.sem, 1)
                pe.wait_ge(enc_in.sem, enc_in.level(b, 32))
                m = 1
                for c in range(DC):
                    for g in range(3):
                        if m >= 2:
                            free(m - 2)
                        for k in range(4):
                            mm = nc.tensor.transpose(ps_t[:, m % 2, k * P:(k + 1) * P],
                                                     enc[:, 4 * g + k, c * P:(c + 1) * P], eye[:, :])
                        mm.then_inc(row_ready.sem, 1)
                        m += 1
                free(m - 2)
                for c in range(DC):
                    mm = nc.tensor.transpose(ps_t[:, 1, c * (REST + 1):c * (REST + 1) + REST],
                                             enc[0:REST, FULL, c * P:(c + 1) * P], eye[0:REST, 0:REST])
                mm.then_inc(row_ready.sem, 1)

            def body(b, n):
                def free(m):
                    pe.wait_ge(lo.sem, lo.level(n, m + 1))

                pe.wait_ge(row_lo.sem, row_lo.level(b, RM))
                pe.wait_ge(w_in_lo.sem, w_in_lo.level(n, 1))
                pe.wait_ge(added.sem, added.level(n, 0))
                for t in range(QT):
                    for c in range(DC):
                        mm = product(ps_m[:, t, :], lambda s: hT[:, s, c, t * P:(t + 1) * P],
                                     lambda s: w_in[:, s, c * HG * DH:(c + 1) * HG * DH], c == 0, c == DC - 1)
                    mm.then_inc(q_ready.sem, 1)
                pe.wait_ge(exped.sem, exped.level(n, 0))
                for j in range(KVJ):
                    if j >= NB:
                        pe.wait_ge(kv_moved.sem, kv_moved.level(n, j - NB + 1))
                    for i, tile in enumerate(range(2 * j, min(2 * j + 2, KT))):
                        rows = P if tile < FULL else REST
                        for c in range(DC):
                            mm = product(ps_s[0:rows, j % NB, i * 2 * DH:(i + 1) * 2 * DH],
                                         lambda s: encT[:, s, c, tile * P:tile * P + rows],
                                         lambda s: w_in[:, s, WQ + c * 2 * DH:WQ + (c + 1) * 2 * DH],
                                         c == 0, c == DC - 1)
                    mm.then_inc(kv_ready.sem, 1)
                for t in range(QT):
                    pe.wait_ge(q_normed.sem, q_normed.level(n, t + 1))
                    for h in range(HG):
                        mm = nc.tensor.transpose(ps_t[:, t, h * P:(h + 1) * P], qn[:, t, h * DH:(h + 1) * DH],
                                                 eye[:, :])
                    mm.then_inc(turned.sem, 1)
                pe.wait_ge(k_normed.sem, k_normed.level(n, 1))
                for m, tiles in enumerate(key_tiles, M_KEYS):
                    free(m - 2)
                    for k, tile in enumerate(tiles):
                        rows = P if tile < FULL else REST
                        mm = nc.tensor.transpose(ps_t[:, m % 2, k * P:k * P + rows], kn[0:rows, tile, :],
                                                 eye[0:rows, 0:rows])
                    mm.then_inc(turned.sem, 1)

                def score(step):
                    h, t = step // QT, step % QT
                    for k in range(NB):
                        if step == 0:
                            free(M_KEYS + k)
                        elif k in (0, 2):
                            pe.wait_ge(exped.sem, exped.level(n, 2 * (step - 1) + k // 2 + 1))
                        a, z = k * BANK, min((k + 1) * BANK, COLS_EVEN)
                        mm = product(ps_s[:, k, 0:z - a], lambda s: qT[:, s, h, t * P:(t + 1) * P],
                                     lambda s: kT[:, s, a:z], True, True)
                        mm.then_inc(scores.sem, 1)

                def turn(step, k):
                    m = M_PROBS + step * JOBS + k
                    if k == 0:
                        pe.wait_ge(normed.sem, normed.level(n, step + 1))
                    free(m - 2)
                    for i, tile in enumerate(key_tiles[k]):
                        rows = P if tile < FULL else REST
                        mm = nc.tensor.transpose(ps_t[0:rows, m % 2, i * P:(i + 1) * P],
                                                 probs[step % 2][:, tile * P:tile * P + rows], eye[:, :])
                    mm.then_inc(turned.sem, 1)

                def weigh(h, tiles):
                    if tiles[0] == 0:
                        free(M_PROBS + (QT * h + QT) * JOBS - 1)
                        if h >= 2:
                            pe.wait_ge(o_lo.sem, o_lo.level(n, h - 1))
                    for tile in tiles:
                        rows = P if tile < FULL else REST
                        mm = product(ps_m[:, h % 2, 0:S], lambda s: v[0:rows, s, tile, :],
                                     lambda s: pT[h % 2][0:rows, s, tile, :], tile == 0, tile == KT - 1)
                    if tiles[-1] == KT - 1:
                        mm.then_inc(o_ready.sem, 1)

                early, late = range(0, 7), range(7, KT)
                for step in range(STEPS + 1):
                    if step < STEPS:
                        score(step)
                    if step > 0:
                        turn(step - 1, 0)
                        turn(step - 1, 1)
                    if step >= 3:
                        weigh((step - 3) // 2, early if step % 2 == 1 else late)
                    if step > 0:
                        turn(step - 1, 2)
                        turn(step - 1, 3)
                weigh(HG - 1, range(KT))
                pe.wait_ge(w_out_lo.sem, w_out_lo.level(n, 1))
                pe.wait_ge(o_lo.sem, o_lo.level(n, HG))
                for t in range(QT):
                    for h in range(HG):
                        mm = product(ps_m[:, 0, t * D:(t + 1) * D], lambda s: oT[:, s, h, t * P:(t + 1) * P],
                                     lambda s: w_out[:, s, h * D:(h + 1) * D], h == 0, h == HG - 1)
                mm.then_inc(y_ready.sem, 1)

            rounds(pe, row, body)


def bit_ffn(nc, x_sb, eye, half_power, w_gate, w_up, w_down, ln_weight):
    TT, D = x_sb.shape[1], x_sb.shape[2]
    I = w_gate.shape[0]
    DC, IC = D // P, I // P
    NB = I // BANK
    EPS, RMS_EPS = 1e-5, 1e-6
    TOP, BOTTOM = 127.0, -128.0
    ROUND = 1.5 * 2.0 ** 23
    K = D * I // P
    W = 3
    TILES = 2
    assert DC == 2 and IC == 8 and NB == 2 and TT == 8

    with ExitStack() as ctx:
        r = Room(nc, ctx, "bf")
        sb, ps, sem, counted = r.sb, r.ps, r.sem, r.counted
        w_raw = sb("w_raw", [P, W, K])
        w_clip = sb("w_clip", [P, W, K])
        w_sign = sb("w_sign", [P, W, K], BF16)
        wT = sb("wT", [P, W, K], BF16)
        abs_sum = sb("abs_sum", [P, W])
        ones = sb("ones", [P, P])
        eye_b = sb("eye_b", [P, P], BF16)
        w_mean = sb("w_mean", [P, W])
        w_scale = sb("w_scale", [P, W])
        ln_w = sb("ln_w", [P, I])
        stats = sb("stats", [P, TT, 6])
        mean_var = sb("mean_var", [P, TT, 2])
        var_eps = sb("var_eps", [P, TT])
        rstd = sb("rstd", [P, TT])
        xn = sb("xn", [P, TT, D])
        x_max = sb("x_max", [P, TT])
        x_inv = sb("x_inv", [P, TT])
        x_scale = sb("x_scale", [P, TT])
        gate_unit = sb("gate_unit", [P, TT])
        up_unit = sb("up_unit", [P, TT])
        xq = sb("xq", [P, TT, D], BF16)
        xqT = sb("xqT", [P, DC, TT * P], BF16)
        silu = [sb(f"silu{i}", [P, I]) for i in range(TILES)]
        h = [sb(f"h{i}", [P, I]) for i in range(TILES)]
        hq = [sb(f"hq{i}", [P, I], BF16) for i in range(TILES)]
        hqT = [sb(f"hqT{i}", [P, IC, P], BF16) for i in range(TILES)]
        h_sq = sb("h_sq", [P, TILES])
        h_var = sb("h_var", [P, TILES])
        h_rstd = sb("h_rstd", [P, TILES])
        h_max = sb("h_max", [P, TILES])
        h_lim = sb("h_lim", [P, TILES])
        h_inv = sb("h_inv", [P, TILES])
        h_scale = sb("h_scale", [P, TILES])
        down_unit = sb("down_unit", [P, TILES])
        ps_g = ps("ps_g", [P, NB, BANK])
        ps_u = ps("ps_u", [P, NB, BANK])
        ps_t = ps("ps_t", [P, 2, 2 * BANK], BF16)
        ps_y = ps("ps_y", [P, TILES, BANK])

        w_in = sem("w_in")
        ln_in = sem("ln_in")
        ones_set = sem("ones_set")
        abs_ready = sem("abs_ready")
        mean_ready = sem("mean_ready")
        prep = sem("prep")
        w_clipped = sem("w_clipped")
        w_signed = sem("w_signed")
        w_turned = sem("w_turned")
        w_here = sem("w_here")
        stat = sem("stat")
        var_ready = sem("var_ready")
        rstd_ready = sem("rstd_ready")
        x_rounded = sem("x_rounded")
        x_quantized = sem("x_quantized")
        x_turned = sem("x_turned")
        x_here = sem("x_here")
        N = TILES
        gu_ready = counted("gu_ready", N)
        silu_ready = counted("silu_ready", N)
        gated = counted("gated", N, before=1)
        squared = counted("squared", N)
        h_var_ready = counted("h_var_ready", N)
        h_rstd_ready = counted("h_rstd_ready", N)
        step = counted("step", 7 * N)
        rounded = counted("rounded", N)
        quantized = counted("quantized", N)
        turned = counted("turned", N)
        here = counted("here", N)
        y_ready = counted("y_ready", N)
        added = counted("added", N, before=1)

        block = ctx.enter_context(nc.Block())

        @block.sync
        def _(sp):
            for n, src in enumerate((w_gate, w_up, w_down)):
                sp.dma_start(w_raw[:, n, :].rearrange("p (a d) -> p a d", d=src.shape[1]),
                             src.rearrange("(a p) d -> p a d", p=P)).then_inc(w_in, 16)
            sp.dma_start(ln_w[:, :], ln_weight.rearrange("(a i) -> a i", a=1).broadcast_to([P, I])
                         ).then_inc(ln_in, 16)

        @block.gpsimd
        def _(pool):
            nc.gpsimd.memset(ones[:, :], 1.0).then_inc(ones_set, 1)
            nc.gpsimd.tensor_copy(eye_b[:, :], eye[:, :]).then_inc(ones_set, 1)
            pool.wait_ge(var_ready, 1)
            nc.gpsimd.tensor_tensor(rstd[:, :], var_eps[:, :], half_power[:, 0:TT], ALU.pow).then_inc(rstd_ready, 1)
            with pool.Fori(0, TT // TILES) as i:
                for k in range(TILES):
                    pool.wait_ge(h_var_ready.sem, h_var_ready.level(i, k + 1))
                    nc.gpsimd.tensor_tensor(h_rstd[:, k:k + 1], h_var[:, k:k + 1], half_power[:, 0:1], ALU.pow
                                            ).then_inc(h_rstd_ready.sem, 1)

        @block.scalar
        def _(act):
            act.wait_ge(x_rounded, 1)
            nc.scalar.activation(xq[:, :, :], xn[:, :, :], ACT.Copy, bias=-ROUND).then_inc(x_quantized, 1)
            for n in range(W):
                act.wait_ge(w_clipped, n + 1)
                nc.scalar.activation(w_sign[:, n, :], w_clip[:, n, :], ACT.Copy, bias=-ROUND).then_inc(w_signed, 1)
            with act.Fori(0, TT // TILES) as i:
                for k in range(TILES):
                    act.wait_ge(gu_ready.sem, gu_ready.level(i, k + 1))
                    act.wait_ge(gated.sem, gated.level(i, 0))
                    nc.scalar.activation(silu[k][:, :], ps_g[:, :, :].rearrange("p n m -> p (n m)"), ACT.Silu,
                                         scale=gate_unit[:, bass.ds(i * TILES + k, 1)]).then_inc(silu_ready.sem, 1)
                    act.wait_ge(gated.sem, gated.level(i, k + 1))
                    nc.scalar.activation(silu[k][:, :], h[k][:, :], ACT.Square, accum_out=h_sq[:, k:k + 1]
                                         ).then_inc(squared.sem, 1)
                    act.wait_ge(rounded.sem, rounded.level(i, k + 1))
                    nc.scalar.activation(hq[k][:, :], h[k][:, :], ACT.Copy, bias=-ROUND).then_inc(quantized.sem, 1)
                    act.wait_ge(turned.sem, turned.level(i, k + 1))
                    nc.scalar.activation(hqT[k][:, :, :].rearrange("p a b -> p (a b)"), ps_t[:, k, :], ACT.Copy
                                         ).then_inc(here.sem, 1)

        @block.vector
        def _(dve):
            count = [0]

            def then(ins):
                count[0] += 1
                ins.then_inc(prep, 1)
                dve.wait_ge(prep, count[0])

            for t in range(TT):
                nc.vector.bn_stats(stats[:, t, :], x_sb[:, t, :]).then_inc(stat, 1)
            dve.wait_ge(stat, TT)
            for t in range(TT):
                nc.vector.bn_aggr(mean_var[:, t, :], stats[:, t, :]).then_inc(stat, 1)
            dve.wait_ge(stat, 2 * TT)
            nc.vector.tensor_scalar(var_eps[:, :], mean_var[:, :, 1], LN_EPS, None, ALU.add).then_inc(var_ready, 1)
            dve.wait_ge(w_in, 16 * W)
            nc.vector.tensor_reduce(abs_sum[:, :], w_raw[:, :, :], AX.X, ALU.add, apply_absolute_value=True
                                    ).then_inc(abs_ready, 1)
            dve.wait_ge(rstd_ready, 1)
            for t in range(TT):
                then(nc.vector.tensor_scalar(xn[:, t, :], x_sb[:, t, :], mean_var[:, t, 0:1], rstd[:, t:t + 1],
                                             ALU.subtract, ALU.mult))
            then(nc.vector.tensor_reduce(x_max[:, :], xn[:, :, :], AX.X, ALU.max, apply_absolute_value=True))
            then(nc.vector.tensor_scalar(x_max[:, :], x_max[:, :], EPS, None, ALU.max))
            then(nc.vector.reciprocal(x_inv[:, :], x_max[:, :]))
            then(nc.vector.tensor_scalar(x_scale[:, :], x_inv[:, :], TOP, None, ALU.mult))
            for t in range(TT):
                then(nc.vector.tensor_scalar(xn[:, t, :], xn[:, t, :], x_scale[:, t:t + 1], TOP, ALU.mult, ALU.min))
            nc.vector.tensor_scalar(xn[:, :, :], xn[:, :, :], BOTTOM, ROUND, ALU.max, ALU.add).then_inc(x_rounded, 1)
            dve.wait_ge(mean_ready, 1)
            then(nc.vector.tensor_scalar(w_mean[:, :], ps_y[:, 0, 0:W], 1.0 / (D * I), EPS, ALU.mult, ALU.max))
            then(nc.vector.reciprocal(w_scale[:, :], w_mean[:, :]))
            for n in range(W):
                then(nc.vector.tensor_scalar(w_clip[:, n, :], w_raw[:, n, :], w_scale[:, n:n + 1], 1.0,
                                             ALU.mult, ALU.min))
                nc.vector.tensor_scalar(w_clip[:, n, :], w_clip[:, n, :], -1.0, ROUND, ALU.max, ALU.add
                                        ).then_inc(w_clipped, 1)
            then(nc.vector.tensor_scalar(gate_unit[:, :], x_max[:, :], w_mean[:, 0:1], 1.0 / TOP, ALU.mult, ALU.mult))
            then(nc.vector.tensor_scalar(up_unit[:, :], x_max[:, :], w_mean[:, 1:2], 1.0 / TOP, ALU.mult, ALU.mult))
            for c in range(DC):
                dve.wait_ge(x_turned, c + 1)
                nc.vector.tensor_copy(xqT[:, c, :], ps_t[:, c, :]).then_inc(x_here, 1)
            for m in range(2 * W):
                dve.wait_ge(w_turned, m + 1)
                nc.vector.tensor_copy(wT[:, m // 2, (m % 2) * I:(m % 2 + 1) * I], ps_t[:, m % 2, :]
                                      ).then_inc(w_here, 1)
            dve.wait_ge(ln_in, 16)
            dve.sem_inc(gated.sem, 1)
            dve.sem_inc(added.sem, 1)
            with dve.Fori(0, TT // TILES) as i:
                for k in range(TILES):
                    n = [7 * k]

                    def next_reads(ins):
                        n[0] += 1
                        ins.then_inc(step.sem, 1)
                        dve.wait_ge(step.sem, step.level(i, n[0]))

                    one = slice(k, k + 1)
                    dve.wait_ge(silu_ready.sem, silu_ready.level(i, k + 1))
                    nc.vector.scalar_tensor_tensor(h[k][:, :], ps_u[:, :, :].rearrange("p n m -> p (n m)"),
                                                   up_unit[:, bass.ds(i * TILES + k, 1)], silu[k][:, :],
                                                   ALU.mult, ALU.mult).then_inc(gated.sem, 1)
                    dve.wait_ge(squared.sem, squared.level(i, k + 1))
                    nc.vector.tensor_scalar(h_var[:, one], h_sq[:, one], 1.0 / I, RMS_EPS, ALU.mult, ALU.add
                                            ).then_inc(h_var_ready.sem, 1)
                    dve.wait_ge(h_rstd_ready.sem, h_rstd_ready.level(i, k + 1))
                    next_reads(nc.vector.scalar_tensor_tensor(h[k][:, :], h[k][:, :], h_rstd[:, one], ln_w[:, :],
                                                              ALU.mult, ALU.mult))
                    next_reads(nc.vector.tensor_reduce(h_max[:, one], h[k][:, :], AX.X, ALU.max,
                                                       apply_absolute_value=True))
                    next_reads(nc.vector.tensor_scalar(h_lim[:, one], h_max[:, one], EPS, None, ALU.max))
                    next_reads(nc.vector.reciprocal(h_inv[:, one], h_lim[:, one]))
                    next_reads(nc.vector.tensor_scalar(h_scale[:, one], h_inv[:, one], TOP, None, ALU.mult))
                    next_reads(nc.vector.tensor_scalar(h[k][:, :], h[k][:, :], h_scale[:, one], TOP,
                                                       ALU.mult, ALU.min))
                    nc.vector.tensor_scalar(h[k][:, :], h[k][:, :], BOTTOM, ROUND, ALU.max, ALU.add
                                            ).then_inc(rounded.sem, 1)
                    next_reads(nc.vector.tensor_scalar(down_unit[:, one], h_lim[:, one], w_mean[:, 2:3], 1.0 / TOP,
                                                       ALU.mult, ALU.mult))
                    dve.wait_ge(y_ready.sem, y_ready.level(i, k + 1))
                    row = x_sb[:, bass.ds(i * TILES + k, 1), :].rearrange("p a d -> p (a d)")
                    nc.vector.scalar_tensor_tensor(row, ps_y[:, k, 0:D], down_unit[:, one], row,
                                                   ALU.mult, ALU.add).then_inc(added.sem, 1)

        @block.tensor
        def _(pe):
            pe.wait_ge(ones_set, 2)
            pe.wait_ge(abs_ready, 1)
            nc.tensor.matmul(ps_y[:, 0, 0:W], ones[:, :], abs_sum[:, :], start=True, stop=True
                             ).then_inc(mean_ready, 1)
            pe.wait_ge(x_quantized, 1)
            for c in range(DC):
                for t in range(TT):
                    mm = nc.tensor.transpose(ps_t[:, c, t * P:(t + 1) * P], xq[:, t, c * P:(c + 1) * P], eye_b[:, :])
                mm.then_inc(x_turned, 1)
            for m in range(2 * W):
                n, half = m // 2, m % 2
                pe.wait_ge(w_signed, n + 1)
                if m < 2:
                    pe.wait_ge(x_here, m + 1)
                else:
                    pe.wait_ge(w_here, m - 1)
                for k in range(IC):
                    if n < 2:
                        src = w_sign[:, n, :].rearrange("p (a d) -> p a d", d=D)[:, k, half * P:(half + 1) * P]
                    else:
                        chunk, o = (half * IC + k) // DC, k % DC
                        src = w_sign[:, n, :].rearrange("p (a i) -> p a i", i=I)[:, o, chunk * P:(chunk + 1) * P]
                    mm = nc.tensor.transpose(ps_t[:, m % 2, k * P:(k + 1) * P], src, eye_b[:, :])
                mm.then_inc(w_turned, 1)
            pe.wait_ge(w_here, 2 * W)
            with pe.Fori(0, TT // TILES) as i:
                for k in range(TILES):
                    pe.wait_ge(gated.sem, gated.level(i, k))
                    for w, bank in ((0, ps_g), (1, ps_u)):
                        for n in range(NB):
                            for c in range(DC):
                                mm = nc.tensor.matmul(bank[:, n, :], xqT[:, c, bass.ds((i * TILES + k) * P, P)],
                                                      wT[:, w, c * I + n * BANK:c * I + (n + 1) * BANK],
                                                      start=c == 0, stop=c == DC - 1)
                    mm.then_inc(gu_ready.sem, 1)
                    pe.wait_ge(quantized.sem, quantized.level(i, k + 1))
                    for c in range(IC):
                        mm = nc.tensor.transpose(ps_t[:, k, c * P:(c + 1) * P], hq[k][:, c * P:(c + 1) * P],
                                                 eye_b[:, :])
                    mm.then_inc(turned.sem, 1)
                    pe.wait_ge(here.sem, here.level(i, k + 1))
                    pe.wait_ge(added.sem, added.level(i, 0))
                    for c in range(IC):
                        mm = nc.tensor.matmul(ps_y[:, k, 0:D], hqT[k][:, c, :], wT[:, 2, c * D:(c + 1) * D],
                                              start=c == 0, stop=c == IC - 1)
                    mm.then_inc(y_ready.sem, 1)


def build(nc, x, ctx_2048, wq, wk, wv, wo, gate_w, wg, wu, wd, cwg, cwu, cwd, wq1, wk1, wv1, wo1, qw, kw,
          w_gate, w_up, w_down, ln_weight, out):
    B, S, D = x.shape
    TT = B * S // P
    with ExitStack() as ctx:
        r = Room(nc, ctx, "all")
        x_sb = r.sb("x", [P, TT, D])
        eye = r.sb("eye", [P, P])
        half_power = r.sb("half_power", [P, 16])
        eye_zero = r.sem("eye_zero")
        stored = r.sem("stored")
        with nc.Block() as block:
            @block.gpsimd
            def _(pool):
                nc.gpsimd.memset(half_power[:, :], -0.5)
                nc.gpsimd.memset(eye[:, :], 0.0).then_inc(eye_zero, 1)
                pool.wait_ge(eye_zero, 1)
                nc.gpsimd.affine_select(out=eye[:, :], in_=eye[:, :], compare_op=ALU.not_equal, fill=1.0, base=0,
                                        pattern=[[-1, P]], channel_multiplier=1)
        cached_attention(nc, x_sb, eye, half_power, x, ctx_2048, wq, wk, wv, wo)
        experts(nc, x_sb, eye, half_power, gate_w, wg, wu, wd, cwg, cwu, cwd)
        grouped_attention(nc, x_sb, eye, half_power, ctx_2048, wq1, wk1, wv1, wo1, qw, kw)
        bit_ffn(nc, x_sb, eye, half_power, w_gate, w_up, w_down, ln_weight)
        with nc.Block() as block:
            @block.sync
            def _(sp):
                sp.dma_start(out.rearrange("b (t p) d -> p (b t) d", p=P), x_sb[:, :, :]).then_inc(stored, 16)
                sp.wait_ge(stored, 16)


_INS = ["x", "ctx_2048", "L0_xattn_wq", "L0_xattn_wk", "L0_xattn_wv", "L0_xattn_wo", "L0_ffn_gate_w",
        "L0_ffn_Wg", "L0_ffn_Wu", "L0_ffn_Wd", "L0_ffn_cWg", "L0_ffn_cWu", "L0_ffn_cWd",
        "L1_xattn_Wq", "L1_xattn_Wk", "L1_xattn_Wv", "L1_xattn_Wo", "L1_xattn_q_norm_w", "L1_xattn_k_norm_w",
        "L1_ffn_w_gate", "L1_ffn_w_up", "L1_ffn_w_down", "L1_ffn_ln_weight"]


def kernel(**inputs):
    import numpy as _np
    import concourse.bacc as _bacc
    from concourse import mybir as _mybir
    from concourse.bass_utils import run_bass_kernel_spmd as _run

    nc = _bacc.Bacc("TRN2", target_bir_lowering=False, num_devices=1)
    arrays, args = {}, []
    for name in _INS:
        a = _np.ascontiguousarray(inputs[name])
        arrays[f"in_{name}"] = a
        args.append(nc.dram_tensor(f"in_{name}", a.shape, _mybir.dt.from_np(a.dtype), kind="ExternalInput").ap())
    args.append(nc.dram_tensor("out_0", (4, 256, 256), _mybir.dt.float32, kind="ExternalOutput").ap())
    build(nc, *args)
    r = _run(nc, [arrays], core_ids=[0])
    return r.results[0]["out_0"]
```

```python
from contextlib import ExitStack

import concourse.bass as bass
from concourse import mybir

ALU = mybir.AluOpType
ACT = mybir.ActivationFunctionType
AX = mybir.AxisListType
F32 = mybir.dt.float32
F32R = mybir.dt.float32r
BF16 = mybir.dt.bfloat16
U32 = mybir.dt.uint32

P = 128
BANK = 512
HI, LO = 0, 1
PARTS = [(HI, HI), (HI, LO), (LO, HI)]

LN_EPS = 1e-5


class Signal:

    def __init__(self, sem, per_round, before=0):
        self.sem, self.per_round, self.before = sem, per_round, before

    def level(self, rnd, k):
        return rnd * self.per_round + (self.before + k)


class Room:

    def __init__(self, nc, ctx, tag):
        self.nc, self.ctx, self.tag = nc, ctx, tag

    def sb(self, name, shape, dt=F32):
        return self.ctx.enter_context(self.nc.sbuf_tensor(f"{self.tag}_{name}", shape, dt))

    def ps(self, name, shape, dt=F32):
        return self.ctx.enter_context(self.nc.psum_tensor(f"{self.tag}_{name}", shape, dt))

    def sem(self, name):
        return self.ctx.enter_context(self.nc.semaphore(f"{self.tag}_{name}"))

    def counted(self, name, per_round, before=0):
        return Signal(self.sem(name), per_round, before)


def f32(ap):
    return ap.bitcast(F32)


def cached_attention(nc, x_sb, eye, half_power, x, kv_cache, wq, wk, wv, wo):
    B, S, D = x.shape
    KV = kv_cache.shape[1]
    DC = D // P
    QT = S // P
    FULL = KV // P
    REST = KV - FULL * P
    KT = FULL + 1
    COLS = KV + S
    COLS_EVEN = COLS + COLS % 2
    TILES = KT + QT
    NB = -(-COLS // BANK)
    SCALE = float(D) ** -0.5
    assert DC == 2 and QT == 2 and FULL == 12 and NB == 4

    with ExitStack() as ctx:
        r = Room(nc, ctx, "ca")
        sb, ps, sem, counted = r.sb, r.ps, r.sem, r.counted
        w_raw = sb("w_raw", [P, 4, DC, D])
        w = sb("w", [P, 4, 2, DC, D], F32R)
        cache = sb("cache", [P, KT, D])
        stats = sb("stats", [P, QT, 6])
        mean_var = sb("mean_var", [P, QT, 2])
        fence = sb("fence", [P, 1])
        var_eps = sb("var_eps", [P, QT])
        rstd = sb("rstd", [P, QT])
        xn = sb("xn", [P, QT, D])
        xnT = sb("xnT", [P, 2, DC, S], F32R)
        qT = sb("qT", [P, 2, DC, S], F32R)
        kT = sb("kT", [P, 2, DC, COLS_EVEN], F32R)
        v = sb("v", [P, 2, TILES, D], F32R)
        probs = sb("probs", [P, QT, COLS])
        pT = sb("pT", [P, 2, TILES, S], F32R)
        oT = sb("oT", [P, 2, DC, S], F32R)
        neg_max = sb("neg_max", [P, QT])
        bias = sb("bias", [P, QT])
        bank_max = sb("bank_max", [P, NB])
        half_sum = sb("half_sum", [P, QT, 2])
        row_sum = sb("row_sum", [P, QT])
        inv_sum = sb("inv_sum", [P, QT])
        ps_s = ps("ps_s", [P, NB, BANK])
        ps_t = ps("ps_t", [P, 2, BANK])
        ps_m = ps("ps_m", [P, 2, BANK])

        def to_blocks(bank, n, m=P):
            return ps_t[:, bank, 0:n * m].rearrange("p (n m) -> p n m", n=n)

        turns = [(ps_t[:, 0, :].rearrange("p (c s) -> p c s", c=DC), lambda s: xnT[:, s, :, :])]
        for c in range(DC):
            for g in range(3):
                at = 4 * g * P
                turns.append((ps_t[:, len(turns) % 2, :], lambda s, c=c, at=at: kT[:, s, c, at:at + 4 * P]))
        turns.append((to_blocks(1, DC, REST + 1)[:, :, 0:REST], lambda s: kT[:, s, :, FULL * P:KV]))
        moves = [(ps_m[:, 0, :].rearrange("p (c s) -> p c s", c=DC), lambda s: qT[:, s, :, :]),
                 (ps_m[:, 1, :].rearrange("p (c s) -> p c s", c=DC), lambda s: kT[:, s, :, KV:COLS]),
                 (ps_m[:, 0, :].rearrange("p (t d) -> p t d", t=QT), lambda s: v[:, s, KT:TILES, :])]
        Q, K, V, M_PROBS = 0, 1, 2, 3
        order = [[0, 1, 2, 3], [4, 5, 6, 7], [8, 9, 10, 11], [12, 13, 14]]
        for t in range(QT):
            for k, tiles in enumerate(order):
                moves.append((to_blocks(k % 2, len(tiles)),
                              lambda s, t=t, a=tiles[0], n=len(tiles): pT[:, s, a:a + n, t * P:(t + 1) * P]))
        M_TURNS = len(moves)
        moves += turns
        output = (ps_m[:, 0, :].rearrange("p (c s) -> p c s", c=DC), lambda s: oT[:, s, :, :])
        M = len(moves) + 1
        TURNS = len(turns)
        HALF = 2 * BANK
        weighs = [(c, tile) for c in range(DC) for tile in range(TILES)]
        SHARE = 3
        assert SHARE * TURNS <= len(weighs)

        x_in = sem("x_in")
        w_in = sem("w_in")
        cache_in = counted("cache_in", 32)
        w_turned = sem("w_turned")
        w_hi = sem("w_hi")
        w_lo = sem("w_lo")
        cleared = sem("cleared")
        ready = counted("ready", M, before=TURNS)
        hi = counted("hi", M, before=TURNS)
        lo = counted("lo", M, before=TURNS)
        v_hi = counted("v_hi", 1)
        v_lo = counted("v_lo", 1)
        stat = counted("stat", 4)
        var_ready = counted("var_ready", 1)
        rstd_ready = counted("rstd_ready", 1)
        xn_ready = counted("xn_ready", 2)
        scores = counted("scores", QT * NB)
        maxed = counted("maxed", 2 * QT)
        biased = counted("biased", QT)
        exped = counted("exped", 2 * QT, before=1)
        summed = counted("summed", 1)
        inverted = counted("inverted", 1)
        y_ready = counted("y_ready", 1)
        added = counted("added", QT, before=1)

        block = ctx.enter_context(nc.Block())

        def rounds(eng, body):
            with eng.Fori(0, B - 1) as b:
                body(b, False)
            body(B - 1, True)

        @block.sync
        def _(sp):
            sp.dma_start(x_sb[:, :, :], x.rearrange("b (t p) d -> p (b t) d", p=P)).then_inc(x_in, 16)
            for n, src in enumerate((wq, wk, wv, wo)):
                sp.dma_start(w_raw[:, n, :, :], src.rearrange("(c p) d -> p c d", p=P)).then_inc(w_in, 16)
            sp.wait_ge(cleared, 3)
            def load_cache(row):
                sp.dma_start(cache[:, 0:FULL, :],
                             row[:, 0:FULL * P, :].rearrange("b (t p) d -> p (b t) d", p=P)
                             ).then_inc(cache_in.sem, 16)
                sp.dma_start(cache[0:REST, FULL, :], row[:, FULL * P:KV, :].rearrange("b p d -> p (b d)")
                             ).then_inc(cache_in.sem, 16)

            load_cache(kv_cache[0:1, :, :])
            with sp.Fori(0, B - 1) as b:
                row = kv_cache[bass.ds(b + 1, 1), :, :]
                sp.wait_ge(v_lo.sem, v_lo.level(b, 1))
                load_cache(row)

        @block.gpsimd
        def _(pool):
            nc.gpsimd.memset(cache[:, FULL, :], 0.0).then_inc(cleared, 1)
            nc.gpsimd.memset(f32(kT[:, :, :, COLS:COLS_EVEN]), 0.0).then_inc(cleared, 1)
            nc.gpsimd.memset(f32(v[:, :, KT - 1, :]), 0.0).then_inc(cleared, 1)
            pool.wait_ge(cleared, 3)

            def token_scale(b):
                pool.wait_ge(var_ready.sem, var_ready.level(b, 1))
                nc.gpsimd.tensor_tensor(rstd[:, :], var_eps[:, :], half_power[:, 0:QT], ALU.pow
                                        ).then_inc(rstd_ready.sem, 1)
            token_scale(0)

            def body(b, last):
                pool.wait_ge(v_hi.sem, v_hi.level(b, 1))
                nc.gpsimd.tensor_tensor(v[:, LO, 0:KT, :], cache[:, :, :], f32(v[:, HI, 0:KT, :]),
                                        ALU.subtract).then_inc(v_lo.sem, 1)
                if not last:
                    token_scale(b + 1)

            rounds(pool, body)

        @block.scalar
        def _(act):
            for n in range(4):
                act.wait_ge(w_turned, n + 1)
                nc.scalar.activation(w[:, n, HI, :, :], ps_s[:, n, :].rearrange("p (c e) -> p c e", c=DC), ACT.Copy
                                     ).then_inc(w_hi, 1)
            act.sem_inc(exped.sem, 1)

            def move_hi(level, src, dst):
                act.wait_ge(ready.sem, level)
                nc.scalar.activation(dst(HI), src, ACT.Copy).then_inc(hi.sem, 1)

            for m in range(TURNS):
                move_hi(m + 1, *turns[m])

            def body(b, last):
                def move(m):
                    move_hi(ready.level(b, m + 1), *moves[m])

                def exp(t, k):
                    if k == 0:
                        act.wait_ge(biased.sem, biased.level(b, t + 1))
                    a, z = ((0, HALF), (HALF, COLS))[k]
                    nc.scalar.activation(probs[:, t, a:z], ps_s[:, :, :].rearrange("p n m -> p (n m)")[:, a:z],
                                         ACT.Exp, bias=bias[:, t:t + 1], scale=SCALE,
                                         accum_out=half_sum[:, t, k:k + 1]).then_inc(exped.sem, 1)

                move(Q)
                move(K)
                act.wait_ge(cache_in.sem, cache_in.level(b, 32))
                nc.scalar.activation(v[:, HI, 0:KT, :], cache[:, :, :], ACT.Copy).then_inc(v_hi.sem, 1)
                exp(0, 0)
                exp(0, 1)
                move(V)
                move(M_PROBS)
                move(M_PROBS + 1)
                exp(1, 0)
                move(M_PROBS + 2)
                exp(1, 1)
                for m in range(M_PROBS + 3, M_TURNS if last else M_TURNS + TURNS):
                    move(m)
                move_hi(ready.level(b, M_TURNS + 1 if last else M), *output)

            rounds(act, body)

        @block.vector
        def _(dve):
            dve.wait_ge(x_in, 16)
            for n in range(4):
                dve.wait_ge(w_hi, n + 1)
                nc.vector.tensor_tensor(w[:, n, LO, :, :], ps_s[:, n, :].rearrange("p (c e) -> p c e", c=DC), f32(w[:, n, HI, :, :]),
                                        ALU.subtract).then_inc(w_lo, 1)
            dve.sem_inc(added.sem, 1)

            def move_lo(level, src, dst):
                dve.wait_ge(hi.sem, level)
                nc.vector.tensor_tensor(dst(LO), src, f32(dst(HI)), ALU.subtract).then_inc(lo.sem, 1)

            def norm(b):
                for t in range(QT):
                    nc.vector.bn_stats(stats[:, t, :], x_sb[:, bass.ds(b * QT + t, 1), :]
                                       .rearrange("p a d -> p (a d)")).then_inc(stat.sem, 1)
                dve.wait_ge(stat.sem, stat.level(b, 2))
                nc.vector.memset(fence[:, :], 0.0)
                for t in range(QT):
                    nc.vector.bn_aggr(mean_var[:, t, :], stats[:, t, :]).then_inc(stat.sem, 1)
                dve.wait_ge(stat.sem, stat.level(b, 4))
                nc.vector.tensor_scalar(var_eps[:, :], mean_var[:, :, 1], LN_EPS, None, ALU.add
                                        ).then_inc(var_ready.sem, 1)
                dve.wait_ge(rstd_ready.sem, rstd_ready.level(b, 1))
                for t in range(QT):
                    nc.vector.tensor_scalar(xn[:, t, :], x_sb[:, bass.ds(b * QT + t, 1), :]
                                            .rearrange("p a d -> p (a d)"), mean_var[:, t, 0:1],
                                            rstd[:, t:t + 1], ALU.subtract, ALU.mult).then_inc(xn_ready.sem, 1)

            norm(0)
            for m in range(TURNS):
                move_lo(m + 1, *turns[m])

            def body(b, last):
                def move(m):
                    move_lo(hi.level(b, m + 1), *moves[m])

                def largest(t, banks):
                    for n in banks:
                        dve.wait_ge(scores.sem, scores.level(b, t * NB + n + 1))
                        last_one = nc.vector.tensor_reduce(bank_max[:, n:n + 1],
                                                           ps_s[:, n, 0:min(BANK, COLS - n * BANK)], AX.X, ALU.max)
                    if banks[-1] == NB - 1:
                        last_one.then_inc(maxed.sem, 1)
                        dve.wait_ge(maxed.sem, maxed.level(b, 2 * t + 1))
                        nc.vector.tensor_reduce(neg_max[:, t:t + 1], bank_max[:, :], AX.X, ALU.max, negate=True
                                                ).then_inc(maxed.sem, 1)
                        dve.wait_ge(maxed.sem, maxed.level(b, 2 * t + 2))
                        nc.vector.tensor_scalar(bias[:, t:t + 1], neg_max[:, t:t + 1], SCALE, None, ALU.mult
                                                ).then_inc(biased.sem, 1)

                move(Q)
                move(K)
                largest(0, range(0, NB))
                move(V)
                largest(1, range(0, 2))
                move(M_PROBS)
                move(M_PROBS + 1)
                largest(1, range(2, NB))
                for m in range(M_PROBS + 2, M_TURNS):
                    move(m)
                nc.vector.tensor_tensor(row_sum[:, :], half_sum[:, :, 0], half_sum[:, :, 1], ALU.add
                                        ).then_inc(summed.sem, 1)
                dve.wait_ge(summed.sem, summed.level(b, 1))
                nc.vector.reciprocal(inv_sum[:, :], row_sum[:, :]).then_inc(inverted.sem, 1)
                if not last:
                    norm(b + 1)
                    for m in range(M_TURNS, M_TURNS + TURNS):
                        move(m)
                move_lo(hi.level(b, M_TURNS + 1 if last else M), *output)
                dve.wait_ge(inverted.sem, inverted.level(b, 1))
                dve.wait_ge(y_ready.sem, y_ready.level(b, 1))
                for t in range(QT):
                    row = x_sb[:, bass.ds(b * QT + t, 1), :].rearrange("p a d -> p (a d)")
                    nc.vector.scalar_tensor_tensor(row, ps_m[:, 1, t * D:(t + 1) * D], inv_sum[:, t:t + 1], row,
                                                   ALU.mult, ALU.add).then_inc(added.sem, 1)

            rounds(dve, body)

        @block.tensor
        def _(pe):
            pe.wait_ge(w_in, 64)
            for n in range(4):
                for c in range(DC):
                    for e in range(DC):
                        mm = nc.tensor.transpose(ps_s[:, n, c * D + e * P:c * D + (e + 1) * P],
                                                 w_raw[:, n, e, c * P:(c + 1) * P], eye[:, :])
                mm.then_inc(w_turned, 1)
            pe.wait_ge(w_lo, 4)

            def product(out, lhs, rhs, first, last):
                for n, (a, c) in enumerate(PARTS):
                    mm = nc.tensor.matmul(out, lhs(a), rhs(c), start=first and n == 0, stop=last and n == 2)
                return mm

            def turn(m, b):
                if m == 0:
                    pe.wait_ge(xn_ready.sem, xn_ready.level(b, 2))
                    for c in range(DC):
                        for t in range(QT):
                            mm = nc.tensor.transpose(ps_t[:, 0, (c * QT + t) * P:(c * QT + t + 1) * P],
                                                     xn[:, t, c * P:(c + 1) * P], eye[:, :])
                elif m < TURNS - 1:
                    if m == 1:
                        pe.wait_ge(cache_in.sem, cache_in.level(b, 32))
                    c, g = (m - 1) // 3, (m - 1) % 3
                    for k in range(4):
                        mm = nc.tensor.transpose(ps_t[:, m % 2, k * P:(k + 1) * P],
                                                 cache[:, 4 * g + k, c * P:(c + 1) * P], eye[:, :])
                else:
                    for c in range(DC):
                        mm = nc.tensor.transpose(ps_t[:, 1, c * (REST + 1):c * (REST + 1) + REST],
                                                 cache[0:REST, FULL, c * P:(c + 1) * P], eye[0:REST, 0:REST])
                mm.then_inc(ready.sem, 1)

            for m in range(TURNS):
                if m >= 2:
                    pe.wait_ge(lo.sem, m - 1)
                turn(m, 0)

            def body(b, last):
                def free(m):
                    pe.wait_ge(lo.sem, lo.level(b, m + 1))

                def project(n, bank):
                    for e in range(DC):
                        for c in range(DC):
                            mm = product(ps_m[:, bank, e * S:(e + 1) * S],
                                         lambda s: w[:, n, s, c, e * P:(e + 1) * P],
                                         lambda s: xnT[:, s, c, :], c == 0, c == DC - 1)
                    mm.then_inc(ready.sem, 1)

                def score(t, banks):
                    for n in banks:
                        if n % 2 == 0:
                            pe.wait_ge(exped.sem, exped.level(b, max(2 * t - 1 + n // 2, 0)))
                        a, z = n * BANK, min((n + 1) * BANK, COLS_EVEN)
                        for c in range(DC):
                            mm = product(ps_s[:, n, 0:z - a], lambda s: qT[:, s, c, t * P:(t + 1) * P],
                                         lambda s: kT[:, s, c, a:z], c == 0, c == DC - 1)
                        mm.then_inc(scores.sem, 1)

                def turn_probs(t, k):
                    m = M_PROBS + t * len(order) + k
                    pe.wait_ge(exped.sem, exped.level(b, 2 * t + k // 2 + 1))
                    if m >= M_PROBS + 2:
                        free(m - 2)
                    for j, tile in enumerate(order[k]):
                        at = tile * P if tile < FULL else (FULL * P if tile == FULL else KV + (tile - KT) * P)
                        n = REST if tile == FULL else P
                        mm = nc.tensor.transpose(ps_t[0:n, k % 2, j * P:(j + 1) * P],
                                                 probs[:, t, at:at + n], eye[:, :])
                    mm.then_inc(ready.sem, 1)

                pe.wait_ge(lo.sem, lo.level(b, 0))
                project(0, 0)
                pe.wait_ge(added.sem, added.level(b, 0))
                project(1, 1)
                free(K)
                score(0, range(0, NB))
                for t in range(QT):
                    for c in range(DC):
                        mm = product(ps_m[:, 0, t * D:(t + 1) * D],
                                     lambda s: xnT[:, s, c, t * P:(t + 1) * P],
                                     lambda s: w[:, 2, s, c, :], c == 0, c == DC - 1)
                mm.then_inc(ready.sem, 1)
                score(1, range(0, 2))
                turn_probs(0, 0)
                turn_probs(0, 1)
                score(1, range(2, NB))
                turn_probs(0, 2)
                turn_probs(0, 3)
                for k in range(len(order)):
                    turn_probs(1, k)
                free(M_TURNS - 1)
                pe.wait_ge(v_lo.sem, v_lo.level(b, 1))
                for i, (c, tile) in enumerate(weighs):
                    if i and i % SHARE == 0 and i // SHARE <= TURNS and not last:
                        m = i // SHARE - 1
                        if m >= 2:
                            free(M_TURNS + m - 2)
                        turn(m, b + 1)
                    n = REST if tile == FULL else P
                    mm = product(ps_m[:, 0, c * S:(c + 1) * S],
                                 lambda s: v[0:n, s, tile, c * P:(c + 1) * P],
                                 lambda s: pT[0:n, s, tile, :], tile == 0, tile == TILES - 1)
                mm.then_inc(ready.sem, 1)
                free(M_TURNS if last else M - 1)
                for t in range(QT):
                    for c in range(DC):
                        mm = product(ps_m[:, 1, t * D:(t + 1) * D], lambda s: oT[:, s, c, t * P:(t + 1) * P],
                                     lambda s: w[:, 3, s, c, :], c == 0, c == DC - 1)
                mm.then_inc(y_ready.sem, 1)

            rounds(pe, body)


def experts(nc, x_sb, eye, half_power, gate_w, wg, wu, wd, cwg, cwu, cwd):
    TT, D = x_sb.shape[1], x_sb.shape[2]
    T = TT * P
    E = gate_w.shape[0]
    I = wg.shape[2]
    CI = cwg.shape[2]
    ROUNDS = cwg.shape[0]
    U = 3
    HALVES = T // BANK
    DC = D // P
    TOP = 4
    MAX8 = 8
    SMALL_SCALE = 0.05
    assert E == 2 * ROUNDS and T == 2 * BANK and CI == P and D == 2 * P
    width = [I, I, CI]
    banks_y = TT * D // BANK

    with ExitStack() as ctx:
        r = Room(nc, ctx, "ex")
        sb, ps, sem, counted = r.sb, r.ps, r.sem, r.counted
        stats = sb("stats", [P, TT, 6])
        mean_var = sb("mean_var", [P, TT, 2])
        var_eps = sb("var_eps", [P, TT])
        rstd = sb("rstd", [P, TT])
        xn = sb("xn", [P, TT, D])
        gate = sb("gate", [E, D])
        gateT = sb("gateT", [P, 2, DC, E], F32R)
        hT = sb("hT", [P, 2, DC, T], F32R)
        logits = sb("logits", [P, TT, E])
        top = sb("top", [P, TT, MAX8])
        top_at = sb("top_at", [P, TT, MAX8], U32)
        top_index = sb("top_index", [P, TT, MAX8])
        above = sb("above", [P, TT, TOP])
        top_exp = sb("top_exp", [P, TT, TOP])
        top_sum = sb("top_sum", [P, TT])
        top_inv = sb("top_inv", [P, TT])
        weight = sb("weight", [P, TT, TOP])
        expert_id = sb("expert_id", [P, E])
        hit = sb("hit", [P, TT, E])
        part = sb("part", [P, TT, E])
        cw = sb("cw", [P, TT, E + ROUNDS])
        cw_unit = [sb(f"cw_unit{u}", [P, TT]) for u in range(U)]
        raw = [sb(f"raw{u}", [P, 2 * DC * width[u] + D]) for u in range(U)]
        w = [sb(f"w{u}", [P, 2, 2 * DC * width[u] + D], F32R) for u in range(U)]
        silu = sb("silu", [P, HALVES, BANK])
        act_gu = sb("act_gu", [P, HALVES, BANK])
        aT = [sb(f"aT{u}", [P, 2, T], F32R) for u in range(U)]
        ps_g = ps("ps_g", [P, HALVES, BANK])
        ps_u = ps("ps_u", [P, HALVES, BANK])
        ps_y = ps("ps_y", [P, banks_y, BANK])

        gate_in = sem("gate_in")
        ids = sem("ids")
        cleared = sem("cleared")
        stat = sem("stat")
        var_ready = sem("var_ready")
        rstd_ready = sem("rstd_ready")
        xn_ready = sem("xn_ready")
        turned = sem("turned")
        turned_hi = sem("turned_hi")
        turned_lo = sem("turned_lo")
        logits_ready = sem("logits_ready")
        logits_here = sem("logits_here")
        above_ready = sem("above_ready")
        exp_ready = sem("exp_ready")
        route = sem("route")
        raw_in = [counted(f"raw_in{u}", 48) for u in range(U)]
        w_hi = [counted(f"w_hi{u}", 1) for u in range(U)]
        w_lo = [counted(f"w_lo{u}", 1) for u in range(U)]
        gate_ready = counted("gate_ready", U * HALVES)
        up_ready = counted("up_ready", U * HALVES)
        silu_ready = counted("silu_ready", U * HALVES)
        a_ready = counted("a_ready", U * HALVES)
        a_hi = counted("a_hi", U * HALVES)
        a_lo = counted("a_lo", U * HALVES)
        cw_ready = counted("cw_ready", U)
        y_ready = counted("y_ready", U * banks_y)
        added = counted("added", U * TT)

        turned_moves = [(ps_y[:, c * HALVES + h, :], lambda s, c=c, h=h: hT[:, s, c, h * BANK:(h + 1) * BANK])
                        for c in range(DC) for h in range(HALVES)]
        turned_moves.append((ps_g[:, 0, 0:DC * E].rearrange("p (c e) -> p c e", c=DC),
                             lambda s: gateT[:, s, :, :]))

        block = ctx.enter_context(nc.Block())

        def rounds(eng, body):
            body(0, True, False)
            with eng.Fori(1, ROUNDS - 1) as i:
                body(i, False, False)
            body(ROUNDS - 1, False, True)

        def turn(i, u):
            return ((u - 1) % U, i + 1 if u > 0 else i)

        @block.sync
        def _(sp):
            sp.dma_start(gate[:, :], gate_w).then_inc(gate_in, 16)

            def load(i, u):
                n = width[u]
                gu = raw[u][:, 0:2 * DC * n].rearrange("p (m c i) -> p m c i", m=2, c=DC)
                for m, src in enumerate(((wg, wu), (wg, wu), (cwg, cwu))[u]):
                    e = 2 * i + u if u < 2 else i
                    sp.dma_start(gu[:, m, :, :], src[bass.ds(e, 1), :, :].rearrange("e (p c) i -> p (e c) i", p=P)
                                 ).then_inc(raw_in[u].sem, 16)
                src = (wd, wd, cwd)[u]
                sp.dma_start(raw[u][0:n, 2 * DC * n:2 * DC * n + D],
                             src[bass.ds(e, 1), :, :].rearrange("e i d -> (e i) d")).then_inc(raw_in[u].sem, 16)

            sp.wait_ge(cleared, 2)
            for u in range(U):
                load(0, u)

            def ahead(i):
                for u in range(U):
                    sp.wait_ge(w_lo[u].sem, w_lo[u].level(i, 0))
                    load(i, u)

            with sp.Fori(1, ROUNDS) as i:
                ahead(i)

        @block.gpsimd
        def _(pool):
            nc.gpsimd.iota(expert_id[:, :], [[1, E]], base=0, channel_multiplier=0,
                           allow_small_or_imprecise_dtypes=True).then_inc(ids, 1)
            for u in range(2):
                nc.gpsimd.memset(raw[u][:, 2 * DC * I:2 * DC * I + D], 0.0).then_inc(cleared, 1)
            pool.wait_ge(var_ready, 1)
            nc.gpsimd.tensor_tensor(rstd[:, :], var_eps[:, :], half_power[:, 0:TT], ALU.pow).then_inc(rstd_ready, 1)

            def w_low(i, u):
                pool.wait_ge(w_hi[u].sem, w_hi[u].level(i, 1))
                nc.gpsimd.tensor_tensor(w[u][:, LO, :], raw[u][:, :], f32(w[u][:, HI, :]), ALU.subtract
                                        ).then_inc(w_lo[u].sem, 1)

            w_low(0, 0)
            w_low(0, 1)

            def body(i, first, last):
                for u in range(U):
                    n = width[u]
                    for h in range(HALVES):
                        pool.wait_ge(a_hi.sem, a_hi.level(i, u * HALVES + h + 1))
                        nc.gpsimd.tensor_tensor(aT[u][0:n, LO, h * BANK:(h + 1) * BANK], act_gu[0:n, h, :],
                                                f32(aT[u][0:n, HI, h * BANK:(h + 1) * BANK]), ALU.subtract
                                                ).then_inc(a_lo.sem, 1)
                    slot, at = turn(i, u)
                    if not (last and u > 0):
                        w_low(at, slot)

            rounds(pool, body)

        @block.scalar
        def _(act):
            for m in range(HALVES * DC + 1):
                act.wait_ge(turned, m + 1)
                src, dst = turned_moves[m]
                nc.scalar.activation(dst(HI), src, ACT.Copy).then_inc(turned_hi, 1)
            act.wait_ge(above_ready, 1)
            nc.scalar.activation(top_exp[:, :, :], above[:, :, :], ACT.Exp).then_inc(exp_ready, 1)

            def w_high(i, u, waits):
                if waits:
                    act.wait_ge(y_ready.sem, y_ready.level(i, (u + 1) * banks_y - U * banks_y))
                act.wait_ge(raw_in[u].sem, raw_in[u].level(i, 48))
                nc.scalar.activation(w[u][:, HI, :], raw[u][:, :], ACT.Copy).then_inc(w_hi[u].sem, 1)

            w_high(0, 0, False)
            w_high(0, 1, False)

            def body(i, first, last):
                for u in range(U):
                    n = width[u]
                    for h in range(HALVES):
                        act.wait_ge(gate_ready.sem, gate_ready.level(i, u * HALVES + h + 1))
                        if not (first and u == 0):
                            act.wait_ge(a_ready.sem, a_ready.level(i, (u - 1) * HALVES + h + 1))
                        nc.scalar.activation(silu[0:n, h, :], ps_g[0:n, h, :], ACT.Silu).then_inc(silu_ready.sem, 1)
                    for h in range(HALVES):
                        if h == 0 and not first:
                            act.wait_ge(y_ready.sem, y_ready.level(i, (u + 1) * banks_y - U * banks_y))
                        act.wait_ge(a_ready.sem, a_ready.level(i, u * HALVES + h + 1))
                        nc.scalar.activation(aT[u][0:n, HI, h * BANK:(h + 1) * BANK], act_gu[0:n, h, :], ACT.Copy
                                             ).then_inc(a_hi.sem, 1)
                    slot, at = turn(i, u)
                    if not (last and u > 0):
                        w_high(at, slot, not (first and u == 0))

            rounds(act, body)

        @block.vector
        def _(dve):
            for t in range(TT):
                nc.vector.bn_stats(stats[:, t, :], x_sb[:, t, :]).then_inc(stat, 1)
            dve.wait_ge(stat, TT)
            for t in range(TT):
                nc.vector.bn_aggr(mean_var[:, t, :], stats[:, t, :]).then_inc(stat, 1)
            dve.wait_ge(stat, 2 * TT)
            nc.vector.tensor_scalar(var_eps[:, :], mean_var[:, :, 1], LN_EPS, None, ALU.add).then_inc(var_ready, 1)
            dve.wait_ge(rstd_ready, 1)
            for t in range(TT):
                nc.vector.tensor_scalar(xn[:, t, :], x_sb[:, t, :], mean_var[:, t, 0:1], rstd[:, t:t + 1],
                                        ALU.subtract, ALU.mult).then_inc(xn_ready, 1)
            for m in range(HALVES * DC + 1):
                dve.wait_ge(turned_hi, m + 1)
                src, dst = turned_moves[m]
                nc.vector.tensor_tensor(dst(LO), src, f32(dst(HI)), ALU.subtract).then_inc(turned_lo, 1)
            dve.wait_ge(logits_ready, 1)
            nc.vector.tensor_copy(logits[:, :, :], ps_y[:, 0, 0:TT * E].rearrange("p (t e) -> p t e", t=TT)
                                  ).then_inc(logits_here, 1)
            dve.wait_ge(logits_here, 1)
            step = [0]

            def then(ins):
                step[0] += 1
                ins.then_inc(route, 1)
                dve.wait_ge(route, step[0])

            for t in range(TT):
                then(nc.vector.max(top[:, t, :], logits[:, t, :]))
                then(nc.vector.max_index(top_at[:, t, :], top[:, t, :], logits[:, t, :]))
            then(nc.vector.tensor_copy(top_index[:, :, :], top_at[:, :, :]))
            nc.vector.tensor_tensor(above[:, :, :], top[:, :, 0:TOP], top[:, :, 0:1].broadcast_to([P, TT, TOP]),
                                    ALU.subtract).then_inc(above_ready, 1)
            dve.wait_ge(exp_ready, 1)
            then(nc.vector.tensor_reduce(top_sum[:, :], top_exp[:, :, :], AX.X, ALU.add))
            then(nc.vector.reciprocal(top_inv[:, :], top_sum[:, :]))
            then(nc.vector.tensor_tensor(weight[:, :, :], top_exp[:, :, :],
                                         top_inv[:, :].unsqueeze(2).broadcast_to([P, TT, TOP]), ALU.mult))
            dve.wait_ge(ids, 1)
            for k in range(TOP):
                then(nc.vector.tensor_tensor(hit[:, :, :], expert_id[:, :].unsqueeze(1).broadcast_to([P, TT, E]),
                                             top_index[:, :, k:k + 1].broadcast_to([P, TT, E]), ALU.is_equal))
                dst = cw[:, :, 0:E] if k == 0 else part[:, :, :]
                then(nc.vector.tensor_tensor(dst, hit[:, :, :], weight[:, :, k:k + 1].broadcast_to([P, TT, E]),
                                             ALU.mult))
                if k:
                    then(nc.vector.tensor_tensor(cw[:, :, 0:E], cw[:, :, 0:E], part[:, :, :], ALU.add))
            pairs = cw[:, :, 0:E].rearrange("p t (c g) -> p t c g", g=2)
            then(nc.vector.tensor_tensor(part[:, :, 0:ROUNDS], pairs[:, :, :, 0], pairs[:, :, :, 1], ALU.add))
            then(nc.vector.tensor_scalar(cw[:, :, E:E + ROUNDS], part[:, :, 0:ROUNDS], SMALL_SCALE, None, ALU.mult))

            def add(i, u):
                for t in range(TT):
                    dve.wait_ge(y_ready.sem, y_ready.level(i, u * banks_y + t // 2 + 1))
                    if t == 0:
                        dve.wait_ge(cw_ready.sem, cw_ready.level(i, u + 1))
                    nc.vector.scalar_tensor_tensor(x_sb[:, t, :], ps_y[:, t // 2, (t % 2) * D:(t % 2 + 1) * D],
                                                   cw_unit[u][:, t:t + 1], x_sb[:, t, :], ALU.mult, ALU.add
                                                   ).then_inc(added.sem, 1)

            def body(i, first, last):
                for u in range(U):
                    n = width[u]
                    e = 2 * i + u if u < 2 else E + i
                    nc.vector.tensor_copy(cw_unit[u][:, :].unsqueeze(2), cw[:, :, bass.ds(e, 1)]
                                          ).then_inc(cw_ready.sem, 1)
                    for h in range(HALVES):
                        if not (first and u == 0):
                            dve.wait_ge(a_lo.sem, a_lo.level(i, (u - 1) * HALVES + h + 1))
                        dve.wait_ge(silu_ready.sem, silu_ready.level(i, u * HALVES + h + 1))
                        dve.wait_ge(up_ready.sem, up_ready.level(i, u * HALVES + h + 1))
                        nc.vector.tensor_tensor(act_gu[0:n, h, :], silu[0:n, h, :], ps_u[0:n, h, :], ALU.mult
                                                ).then_inc(a_ready.sem, 1)
                    if u > 0:
                        add(i, u - 1)
                    elif not first:
                        add(i - 1, U - 1)

            rounds(dve, body)
            add(ROUNDS - 1, U - 1)

        @block.tensor
        def _(pe):
            def product(out, lhs, rhs, first, last):
                for n, (a, c) in enumerate(PARTS):
                    mm = nc.tensor.matmul(out, lhs(a), rhs(c), start=first and n == 0, stop=last and n == 2)
                return mm

            pe.wait_ge(xn_ready, TT)
            for c in range(DC):
                for h in range(HALVES):
                    for k in range(4):
                        mm = nc.tensor.transpose(ps_y[:, c * HALVES + h, k * P:(k + 1) * P],
                                                 xn[:, 4 * h + k, :].rearrange("p (q c) -> p q c", c=DC)[:, :, c],
                                                 eye[:, :])
                    mm.then_inc(turned, 1)
            pe.wait_ge(gate_in, 16)
            for c in range(DC):
                mm = nc.tensor.transpose(ps_g[:, 0, c * E:(c + 1) * E],
                                         gate[:, :].rearrange("e (q c) -> e q c", c=DC)[:, :, c], eye[0:E, 0:E])
            mm.then_inc(turned, 1)
            pe.wait_ge(turned_lo, HALVES * DC + 1)
            for t in range(TT):
                for c in range(DC):
                    mm = product(ps_y[:, 0, t * E:(t + 1) * E], lambda s: hT[:, s, c, t * P:(t + 1) * P],
                                 lambda s: gateT[:, s, c, :], c == 0, c == DC - 1)
            mm.then_inc(logits_ready, 1)
            pe.wait_ge(logits_here, 1)

            def gate_up(i, u, first):
                n = width[u]
                pe.wait_ge(w_lo[u].sem, w_lo[u].level(i, 1))
                for h in range(HALVES):
                    if not first:
                        pe.wait_ge(a_ready.sem, a_ready.level(i, (u - 1) * HALVES + h + 1))
                    for m, (bank, done) in enumerate(((ps_g, gate_ready), (ps_u, up_ready))):
                        for c in range(DC):
                            mm = product(bank[0:n, h, :], lambda s: w[u][:, s, (m * DC + c) * n:(m * DC + c + 1) * n],
                                         lambda s: hT[:, s, c, h * BANK:(h + 1) * BANK], c == 0, c == DC - 1)
                        mm.then_inc(done.sem, 1)

            def down(i, u, first):
                n = width[u]
                for t in range(TT):
                    if t % 4 == 0:
                        pe.wait_ge(a_lo.sem, a_lo.level(i, u * HALVES + t // 4 + 1))
                    if not first and t % 2 == 0:
                        pe.wait_ge(added.sem, added.level(i, (u - 1) * TT + t + 2))
                    mm = product(ps_y[:, t // 2, (t % 2) * D:(t % 2 + 1) * D],
                                 lambda s: aT[u][0:n, s, t * P:(t + 1) * P],
                                 lambda s: w[u][0:n, s, 2 * DC * n:2 * DC * n + D], True, True)
                    if t % 2 == 1:
                        mm.then_inc(y_ready.sem, 1)

            def body(i, first, last):
                for u in range(U):
                    gate_up(i, u, first and u == 0)
                    if u > 0:
                        down(i, u - 1, first and u == 1)
                    elif not first:
                        down(i - 1, U - 1, False)

            rounds(pe, body)
            down(ROUNDS - 1, U - 1, False)


def grouped_attention(nc, x_sb, eye, half_power, encoder, wq, wk, wv, wo, q_norm_w, k_norm_w):
    TT, D = x_sb.shape[1], x_sb.shape[2]
    B, KV, _ = encoder.shape
    QT = TT // B
    S = QT * P
    DH = q_norm_w.shape[0]
    G = wk.shape[1] // DH
    HG = wq.shape[1] // (G * DH)
    DC = D // P
    FULL = KV // P
    REST = KV - FULL * P
    KT = FULL + 1
    COLS_EVEN = KV + KV % 2
    NB = -(-KV // BANK)
    RMS_EPS = 1e-6
    STEPS = HG * QT
    KVJ = (KT + 1) // 2
    ENCJ = 6 + DC
    TB = 3
    K_EARLY = 8
    WQ, WKV, WO = DC * HG * DH, DC * 2 * DH, HG * D
    assert DH == P and DC == 2 and QT == 2 and HG == 4 and G == 4 and NB == 4 and FULL == 12
    HALF = 2 * BANK
    key_tiles = [range(0, 4), range(4, 8), range(8, 12), range(12, 13)]
    JOBS = len(key_tiles)

    RING = ("xT", "encT", "q", "kv", "qT", "kT", "pT", "y")
    ROW = [("encT", m, G) for m in (0, 3, 1, 4, 2, 5, 6, 7)]

    def step_plan(n, last):
        g, s = n // STEPS, n % STEPS
        turn = [("pT", (n - 1) * JOBS + k, 0) for k in range(JOBS)] if 1 <= n <= STEPS * G else []
        more, to = [], g + 1
        if n < STEPS * G and not (last and g == G - 1):
            more = {0: [("q", 0, to), ("q", 1, to), ("q_eps", 0, to)],
                    2: [("kv", 0, to), ("kv", 1, to), ("kv", 2, to)],
                    3: [("qT", 0, to), ("qT", 1, to)],
                    4: [("kv", 3, to), ("k_eps", 0, to), ("kv", 4, to)],
                    5: [("kT", 0, to), ("kT", 1, to)],
                    6: [("kv", 5, to), ("kv", 6, to), ("k_eps", 1, to)],
                    7: [("kT", 2, to), ("kT", 3, to)]}.get(s, [])
        if s == 4 and 0 < g < G:
            more = [("y", g - 1, 0)] + more
        if not last:
            more = more + {(G - 2, 5): [("norm", 0, G)], (G - 2, 6): ROW[:2], (G - 2, 7): [("xT", 0, G)] + ROW[2:4],
                           (G - 1, 0): ROW[4:6], (G - 1, 1): ROW[6:]}.get((g, s), [])
        out = []
        while turn or more:
            if turn:
                out.append(turn.pop(0))
            if more:
                out.append(more.pop(0))
        return out

    PROLOGUE = ([("norm", 0, 0)] + [("encT", m, 0) for m in range(ENCJ)] + [("xT", 0, 0)]
                + [("q", 0, 0), ("q", 1, 0), ("q_eps", 0, 0)] + [("kv", j, 0) for j in range(4)]
                + [("k_eps", 0, 0)] + [("kv", j, 0) for j in range(4, KVJ)]
                + [("k_eps", 1, 0), ("qT", 0, 0), ("qT", 1, 0), ("kT", 0, 0), ("kT", 1, 0),
                   ("kT", 2, 0), ("kT", 3, 0)])
    N_STEPS = STEPS * G
    DRAIN = 3
    EXP_AT = (1, 2)
    IN_PARTS = ((0, WQ), (WQ, WQ + WKV))
    SPLIT_AT = (1, 7)
    plans = {last: [step_plan(n, last) for n in range(N_STEPS + DRAIN)] for last in (False, True)}
    for last in plans:
        plans[last][-1].append(("y", G - 1, 0))

    def places(entries):
        at, n, a = {}, 0, 0
        for e in entries:
            if e[0] in RING:
                a += e[0] != "y"
                at[e] = (n, a)
                n += 1
        return at, n, a

    pro_at, PRO, PRO_ACT = places(PROLOGUE)
    body_at, BODY, BODY_ACT = places([e for p in plans[False] for e in p])
    last_at, _, _ = places([e for p in plans[True] for e in p])
    assert BODY % TB == 0

    with ExitStack() as ctx:
        r = Room(nc, ctx, "ga")
        sb, ps, sem, counted = r.sb, r.ps, r.sem, r.counted
        w_in_raw = sb("w_in_raw", [P, WQ + WKV])
        w_in = sb("w_in", [P, 2, WQ + WKV], F32R)
        w_out_raw = sb("w_out_raw", [P, WO])
        w_out = sb("w_out", [P, 2, WO], F32R)
        norm_w = sb("norm_w", [P, 2])
        qk_w = sb("qk_w", [P, 1])
        fence = sb("fence", [P, 1])
        enc = sb("enc", [P, KT, D])
        encT = sb("encT", [P, 2, DC, COLS_EVEN], F32R)
        stats = sb("stats", [P, QT, 6])
        mean_var = sb("mean_var", [P, QT, 2])
        var_eps = sb("var_eps", [P, QT])
        rstd = sb("rstd", [P, QT])
        hT = sb("hT", [P, 2, DC, S], F32R)
        q_sq = sb("q_sq", [P, QT * HG])
        q_sq_eps = sb("q_sq_eps", [P, QT * HG])
        q_scale = sb("q_scale", [P, QT * HG])
        k_sq = sb("k_sq", [P, KT])
        k_sq_eps = sb("k_sq_eps", [P, KT])
        k_scale = sb("k_scale", [P, KT])
        qn = sb("qn", [P, QT, HG * DH])
        xn = qn[:, :, 0:D]
        kn = sb("kn", [P, KT, DH])
        qT = [sb(f"qT{i}", [P, 2, HG, S], F32R) for i in range(2)]
        kT = [sb(f"kT{i}", [P, 2, COLS_EVEN], F32R) for i in range(2)]
        v = [sb(f"v{i}", [P, 2, KT, DH], F32R) for i in range(2)]
        probs = [sb(f"probs{i}", [P, KV]) for i in range(2)]
        bank_max = sb("bank_max", [P, NB])
        neg_max = sb("neg_max", [P, 2])
        half_sum = sb("half_sum", [P, 2, 2])
        row_sum = sb("row_sum", [P, 1])
        inv_sum = sb("inv_sum", [P, 4])
        inv_rows = sb("inv_rows", [P, S])
        out_n = sb("out_n", [P, S])
        pT = sb("pT", [P, 2, KT, S], F32R)
        oT = sb("oT", [P, 2, HG, S], F32R)
        ps_s = ps("ps_s", [P, NB, BANK])
        ps_t = ps("ps_t", [P, TB, BANK])
        ps_m = ps("ps_m", [P, 2, S])

        cleared = sem("cleared")
        norm_in = sem("norm_in")
        qk_ready = sem("qk_ready")
        R = B * G
        w_q_in = counted("w_q_in", 16)
        w_kv_in = counted("w_kv_in", 32)
        w_out_in = counted("w_out_in", 16)
        w_in_hi = counted("w_in_hi", 2)
        w_in_lo = counted("w_in_lo", 2)
        w_out_hi = counted("w_out_hi", 1)
        w_out_lo = counted("w_out_lo", 1)
        enc_in = counted("enc_in", 32)
        stat = counted("stat", 4)
        var_ready = counted("var_ready", 1)
        rstd_ready = counted("rstd_ready", 1)
        xn_ready = counted("xn_ready", 1)
        q_eps = counted("q_eps", 1)
        q_scaled = counted("q_scaled", 1)
        q_normed = counted("q_normed", 1)
        k_eps = counted("k_eps", 2)
        k_scaled = counted("k_scaled", 2)
        k_normed = counted("k_normed", 2)
        full = counted("full", BODY, before=PRO)
        read = counted("read", BODY_ACT, before=PRO_ACT)
        empty = counted("empty", BODY, before=PRO)
        scores = counted("scores", N_STEPS * NB)
        maxed = counted("maxed", N_STEPS)
        neg_ready = counted("neg_ready", N_STEPS)
        exped = counted("exped", 2 * N_STEPS)
        summed = counted("summed", N_STEPS)
        inverted = counted("inverted", N_STEPS)
        UNITS = N_STEPS // QT
        out_ready = counted("out_ready", UNITS)
        inv_here = counted("inv_here", UNITS)
        out_here = counted("out_here", UNITS)
        out_hi = counted("out_hi", UNITS)
        out_lo = counted("out_lo", UNITS)

        block = ctx.enter_context(nc.Block())

        class Rows:

            def __init__(self, b, last):
                self.b, self.last, self.at = b, last, last_at if last else body_at

            def place(self, e):
                return self.at[e][0]

            def bank(self, e):
                return (self.at[e][0] + PRO) % TB

            def full(self, e):
                return full.sem, full.level(self.b, self.at[e][0] + 1)

            def read(self, e):
                return read.sem, read.level(self.b, self.at[e][1])

            def empty(self, e):
                return empty.sem, empty.level(self.b, self.at[e][0] + 1)

            def before(self, e):
                return empty.sem, empty.level(self.b, self.at[e][0] - TB + 1)

        class Start(Rows):

            def __init__(self):
                self.b, self.last, self.at = 0, False, pro_at

            def bank(self, e):
                return self.at[e][0] % TB

            def full(self, e):
                return full.sem, self.at[e][0] + 1

            def read(self, e):
                return read.sem, self.at[e][1]

            def empty(self, e):
                return empty.sem, self.at[e][0] + 1

            def before(self, e):
                return empty.sem, self.at[e][0] - TB + 1

        def rows(eng, body):
            with eng.Fori(0, B - 1) as b:
                body(b, False)
            body(B - 1, True)

        def enc_block(m):
            return [(4 * (m % 3) + k, m // 3) for k in range(4)] if m < 6 else [(FULL, m - 6)]

        def kv_tiles(j):
            tiles = range(2 * j, min(2 * j + 2, KT))
            return tiles, P if tiles[-1] < FULL else REST

        def ring_parts(e, bank, p):
            kind, m, _ = e
            src = ps_t[:, bank, :]
            if kind == "xT":
                return src.rearrange("p (c s) -> p c s", c=DC), lambda s: hT[:, s, :, :]
            if kind == "encT":
                if m < 6:
                    at = 4 * (m % 3) * P
                    return src, lambda s: encT[:, s, m // 3, at:at + 4 * P]
                return src[:, 0:REST], lambda s: encT[:, s, m - 6, FULL * P:KV]
            if kind == "qT":
                return (src.rearrange("p (h s) -> p h s", h=HG),
                        lambda s: qT[p][:, s, :, m * P:(m + 1) * P])
            if kind == "kT":
                a = key_tiles[m][0] * P
                n = P * len(key_tiles[m]) if m < JOBS - 1 else REST
                return src[:, 0:n], lambda s: kT[p][:, s, a:a + n]
            step, k = m // JOBS, m % JOBS
            t, a, n = step % QT, key_tiles[k][0], len(key_tiles[k])
            top = P if a < FULL else REST
            return (src[0:top, 0:n * P].rearrange("p (k s) -> p k s", k=n),
                    lambda s: pT[0:top, s, a:a + n, t * P:(t + 1) * P])

        @block.sync
        def _(sp):
            sp.dma_start(norm_w[:, 0:1], q_norm_w.rearrange("(p a) -> p a", a=1)).then_inc(norm_in, 16)
            sp.dma_start(norm_w[:, 1:2], k_norm_w.rearrange("(p a) -> p a", a=1)).then_inc(norm_in, 16)
            sp.wait_ge(cleared, 5)

            def load_encoder(b):
                row = encoder[bass.ds(b, 1), :, :]
                sp.dma_start(enc[:, 0:FULL, :], row[:, 0:FULL * P, :].rearrange("b (t p) d -> p (b t) d", p=P)
                             ).then_inc(enc_in.sem, 16)
                sp.dma_start(enc[0:REST, FULL, :], row[:, FULL * P:KV, :].rearrange("b p d -> p (b d)")
                             ).then_inc(enc_in.sem, 16)

            def load_q(g):
                sp.dma_start(w_in_raw[:, 0:WQ].rearrange("p (c e) -> p c e", c=DC),
                             wq.rearrange("(c p) e -> p c e", p=P)[:, :, g * HG * DH:(g + 1) * HG * DH]
                             ).then_inc(w_q_in.sem, 16)

            def load_kv(g):
                kv = w_in_raw[:, WQ:WQ + WKV].rearrange("p (c m e) -> p c m e", c=DC, m=2)
                for m, src in enumerate((wk, wv)):
                    sp.dma_start(kv[:, :, m, :], src.rearrange("(c p) e -> p c e", p=P)[:, :, g * DH:(g + 1) * DH]
                                 ).then_inc(w_kv_in.sem, 16)

            def load_out(g):
                sp.dma_start(w_out_raw[:, :].rearrange("p (h d) -> p h d", h=HG),
                             wo[g * HG * DH:(g + 1) * HG * DH, :].rearrange("(h p) d -> p h d", p=P)
                             ).then_inc(w_out_in.sem, 16)

            load_encoder(0)
            load_q(0)
            load_kv(0)
            load_out(0)
            sp.wait_ge(w_in_lo.sem, 1)
            load_q(1)
            sp.wait_ge(w_in_lo.sem, 2)
            load_kv(1)

            def body(b, last):
                if not last:
                    sp.wait_ge(full.sem, full.level(b, 0))
                    load_encoder(b + 1)
                for g in range(G):
                    n = b * G + g
                    if not (last and g >= G - 2):
                        sp.wait_ge(w_in_lo.sem, w_in_lo.level(n + 1, 1))
                        load_q((g + 2) % G)
                        sp.wait_ge(w_in_lo.sem, w_in_lo.level(n + 1, 2))
                        load_kv((g + 2) % G)
                    if not (last and g == G - 1):
                        sp.wait_ge(w_out_lo.sem, w_out_lo.level(n, 1))
                        load_out((g + 1) % G)

            rows(sp, body)

        @block.gpsimd
        def _(pool):
            nc.gpsimd.memset(kn[:, FULL, :], 0.0).then_inc(cleared, 1)
            nc.gpsimd.memset(k_sq[:, FULL:KT], 1.0).then_inc(cleared, 1)
            for i in range(2):
                nc.gpsimd.memset(f32(kT[i][:, :, KV:COLS_EVEN]), 0.0).then_inc(cleared, 1)
            nc.gpsimd.memset(fence[:, :], 0.0).then_inc(cleared, 1)

            def split_in(n, k):
                pool.wait_ge(w_in_hi.sem, w_in_hi.level(n, k + 1))
                a, z = IN_PARTS[k]
                nc.gpsimd.tensor_tensor(w_in[:, LO, a:z], w_in_raw[:, a:z], f32(w_in[:, HI, a:z]), ALU.subtract
                                        ).then_inc(w_in_lo.sem, 1)

            def small(e, b, n):
                kind, m, _ = e
                if kind == "norm":
                    pool.wait_ge(var_ready.sem, var_ready.level(b, 1))
                    nc.gpsimd.tensor_tensor(rstd[:, :], var_eps[:, :], half_power[:, 0:QT], ALU.pow
                                            ).then_inc(rstd_ready.sem, 1)
                if kind == "q_eps":
                    pool.wait_ge(q_eps.sem, q_eps.level(n, 1))
                    nc.gpsimd.tensor_tensor(q_scale[:, :], q_sq_eps[:, :], half_power[:, 0:QT * HG], ALU.pow
                                            ).then_inc(q_scaled.sem, 1)
                    pool.wait_ge(q_scaled.sem, q_scaled.level(n, 1))
                    heads = qn[:, :, :].rearrange("p t (h d) -> p (t h) d", d=DH)
                    nc.gpsimd.tensor_tensor(heads, heads, q_scale[:, :].unsqueeze(2)
                                            .broadcast_to([P, QT * HG, DH]), ALU.mult).then_inc(q_normed.sem, 1)
                if kind == "k_eps":
                    a, z = ((0, K_EARLY), (K_EARLY, KT))[m]
                    pool.wait_ge(k_eps.sem, k_eps.level(n, m + 1))
                    nc.gpsimd.tensor_tensor(k_scale[:, a:z], k_sq_eps[:, a:z], half_power[:, 0:z - a], ALU.pow
                                            ).then_inc(k_scaled.sem, 1)
                    pool.wait_ge(k_scaled.sem, k_scaled.level(n, m + 1))
                    nc.gpsimd.tensor_tensor(kn[:, a:z, :], kn[:, a:z, :], k_scale[:, a:z].unsqueeze(2)
                                            .broadcast_to([P, z - a, DH]), ALU.mult).then_inc(k_normed.sem, 1)

            split_in(0, 0)
            split_in(0, 1)
            for e in PROLOGUE:
                small(e, 0, 0)
            split_in(1, 0)
            split_in(1, 1)

            def body(b, last):
                for n in range(N_STEPS + DRAIN):
                    g, s = n // STEPS, n % STEPS
                    for e in plans[last][n]:
                        small(e, b + 1, b * G + e[2])
                    if n >= 4 and n % 2 == 0:
                        u = (n - 4) // 2
                        pool.wait_ge(out_hi.sem, out_hi.level(b, u + 1))
                        nc.gpsimd.tensor_tensor(oT[:, LO, u % HG, :], out_n[:, :], f32(oT[:, HI, u % HG, :]),
                                                ALU.subtract).then_inc(out_lo.sem, 1)
                    if s in SPLIT_AT and g < G and not (last and g >= G - 2):
                        split_in(b * G + g + 2, SPLIT_AT.index(s))
                    if s == 5 and g < G:
                        pool.wait_ge(w_out_hi.sem, w_out_hi.level(b * G + g, 1))
                        nc.gpsimd.tensor_tensor(w_out[:, LO, :], w_out_raw[:, :], f32(w_out[:, HI, :]), ALU.subtract
                                                ).then_inc(w_out_lo.sem, 1)

            rows(pool, body)

        @block.scalar
        def _(act):
            def split_in(n, k):
                if k == 0:
                    act.wait_ge(w_q_in.sem, w_q_in.level(n, 16))
                else:
                    act.wait_ge(w_kv_in.sem, w_kv_in.level(n, 32))
                a, z = IN_PARTS[k]
                nc.scalar.activation(w_in[:, HI, a:z], w_in_raw[:, a:z], ACT.Copy).then_inc(w_in_hi.sem, 1)

            def ring(rows_, e, p):
                kind, m, _ = e
                if kind not in RING or kind == "y":
                    return
                act.wait_ge(*rows_.full(e))
                bank = rows_.bank(e)
                if kind == "q":
                    for h in range(HG):
                        last_one = nc.scalar.activation(qn[:, m, h * DH:(h + 1) * DH],
                                                        ps_t[:, bank, h * DH:(h + 1) * DH], ACT.Square,
                                                        accum_out=q_sq[:, m * HG + h:m * HG + h + 1])
                elif kind == "kv":
                    tiles, top = kv_tiles(m)
                    src = ps_t[0:top, bank, 0:len(tiles) * 2 * DH].rearrange("p (t m d) -> p t m d", m=2, d=DH)
                    for i, tile in enumerate(tiles):
                        nc.scalar.activation(kn[0:top, tile, :], src[:, i, 0, :], ACT.Square,
                                             accum_out=k_sq[0:top, tile:tile + 1])
                    last_one = nc.scalar.activation(v[p][0:top, HI, tiles[0]:tiles[-1] + 1, :], src[:, :, 1, :],
                                                    ACT.Copy)
                else:
                    src, dst = ring_parts(e, bank, p)
                    scale = qk_w[:, 0:1] if kind == "kT" else 1.0
                    last_one = nc.scalar.activation(dst(HI), src, ACT.Copy, scale=scale)
                last_one.then_inc(read.sem, 1)

            split_in(0, 0)
            split_in(0, 1)
            act.wait_ge(qk_ready, 1)
            start = Start()
            for e in PROLOGUE:
                ring(start, e, 0)
            split_in(1, 0)
            split_in(1, 1)

            def body(b, last):
                row = Rows(b, last)

                def exp(n, k):
                    if k == 0:
                        act.wait_ge(neg_ready.sem, neg_ready.level(b, n + 1))
                    a, z = ((0, HALF), (HALF, KV))[k]
                    nc.scalar.activation(probs[n % 2][:, a:z],
                                         ps_s[:, :, :].rearrange("p n m -> p (n m)")[:, a:z], ACT.Exp,
                                         bias=neg_max[:, n % 2:n % 2 + 1],
                                         accum_out=half_sum[:, n % 2, k:k + 1]).then_inc(exped.sem, 1)

                for n in range(N_STEPS + DRAIN):
                    g, s = n // STEPS, n % STEPS
                    plan = plans[last][n]
                    u = (n - 4) // 2
                    with_out = n >= 4 and n % 2 == 0
                    if with_out:
                        act.wait_ge(out_ready.sem, out_ready.level(b, u + 1))
                        nc.scalar.activation(inv_rows[:, :], ps_m[:, 1, :], ACT.Copy
                                             ).then_inc(inv_here.sem, 1)
                    jobs = [e for e in plan if e[0] in RING and e[0] != "y"]
                    a, z = EXP_AT
                    for e in jobs[:a]:
                        ring(row, e, e[2] % 2)
                    if n < N_STEPS:
                        exp(n, 0)
                    for e in jobs[a:z]:
                        ring(row, e, e[2] % 2)
                    if n < N_STEPS:
                        exp(n, 1)
                    for e in jobs[z:]:
                        ring(row, e, e[2] % 2)
                    if with_out:
                        act.wait_ge(out_here.sem, out_here.level(b, u + 1))
                        if g and u % HG == 0:
                            act.wait_ge(*row.full(("y", g - 1, 0)))
                        nc.scalar.activation(oT[:, HI, u % HG, :], out_n[:, :], ACT.Copy).then_inc(out_hi.sem, 1)
                    if s in SPLIT_AT and g < G and not (last and g >= G - 2):
                        split_in(b * G + g + 2, SPLIT_AT.index(s))
                    if s == 5 and g < G:
                        if g:
                            act.wait_ge(*row.full(("y", g - 1, 0)))
                        act.wait_ge(w_out_in.sem, w_out_in.level(b * G + g, 16))
                        nc.scalar.activation(w_out[:, HI, :], w_out_raw[:, :], ACT.Copy).then_inc(w_out_hi.sem, 1)

            rows(act, body)

        @block.vector
        def _(dve):
            dve.wait_ge(norm_in, 32)
            nc.vector.tensor_tensor(qk_w[:, :], norm_w[:, 0:1], norm_w[:, 1:2], ALU.mult).then_inc(qk_ready, 1)
            dve.wait_ge(cleared, 5)

            def norm(b):
                for t in range(QT):
                    nc.vector.bn_stats(stats[:, t, :], x_sb[:, bass.ds(b * QT + t, 1), :]
                                       .rearrange("p a d -> p (a d)")).then_inc(stat.sem, 1)
                dve.wait_ge(stat.sem, stat.level(b, QT))
                nc.vector.memset(fence[:, :], 0.0)
                for t in range(QT):
                    nc.vector.bn_aggr(mean_var[:, t, :], stats[:, t, :]).then_inc(stat.sem, 1)
                dve.wait_ge(stat.sem, stat.level(b, 2 * QT))
                nc.vector.tensor_scalar(var_eps[:, :], mean_var[:, :, 1], LN_EPS, None, ALU.add
                                        ).then_inc(var_ready.sem, 1)
                dve.wait_ge(rstd_ready.sem, rstd_ready.level(b, 1))
                for t in range(QT):
                    last_one = nc.vector.tensor_scalar(xn[:, t, :], x_sb[:, bass.ds(b * QT + t, 1), :]
                                                       .rearrange("p a d -> p (a d)"), mean_var[:, t, 0:1],
                                                       rstd[:, t:t + 1], ALU.subtract, ALU.mult)
                last_one.then_inc(xn_ready.sem, 1)

            def entry(rows_, e, b, b_next, n):
                kind, m, _ = e
                p = e[2] % 2
                if kind == "norm":
                    norm(b_next)
                elif kind == "q_eps":
                    nc.vector.tensor_scalar(q_sq_eps[:, :], q_sq[:, :], DH * RMS_EPS, None, ALU.add
                                            ).then_inc(q_eps.sem, 1)
                elif kind == "k_eps":
                    a, z = ((0, K_EARLY), (K_EARLY, KT))[m]
                    nc.vector.tensor_scalar(k_sq_eps[:, a:z], k_sq[:, a:z], 1.0 / DH, RMS_EPS, ALU.mult, ALU.add
                                            ).then_inc(k_eps.sem, 1)
                elif kind == "y":
                    dve.wait_ge(*rows_.full(e))
                    tokens = x_sb[:, bass.ds(b * QT, QT), :]
                    nc.vector.tensor_tensor(tokens, tokens, ps_t[:, rows_.bank(e), :]
                                            .rearrange("p (t d) -> p t d", t=QT), ALU.add).then_inc(empty.sem, 1)
                else:
                    dve.wait_ge(*rows_.read(e))
                    bank = rows_.bank(e)
                    if kind == "q":
                        ins = nc.vector.tensor_copy(qn[:, m, :], ps_t[:, bank, :])
                    elif kind == "kv":
                        tiles, top = kv_tiles(m)
                        src = ps_t[0:top, bank, 0:len(tiles) * 2 * DH].rearrange("p (t m d) -> p t m d", m=2, d=DH)
                        at = slice(tiles[0], tiles[-1] + 1)
                        nc.vector.tensor_copy(kn[0:top, at, :], src[:, :, 0, :])
                        ins = nc.vector.tensor_tensor(v[p][0:top, LO, at, :], src[:, :, 1, :],
                                                      f32(v[p][0:top, HI, at, :]), ALU.subtract)
                    elif kind == "kT":
                        src, dst = ring_parts(e, bank, p)
                        ins = nc.vector.scalar_tensor_tensor(dst(LO), src, qk_w[:, 0:1], f32(dst(HI)),
                                                             ALU.mult, ALU.subtract)
                    else:
                        src, dst = ring_parts(e, bank, p)
                        ins = nc.vector.tensor_tensor(dst(LO), src, f32(dst(HI)), ALU.subtract)
                    ins.then_inc(empty.sem, 1)

            start = Start()
            for e in PROLOGUE:
                entry(start, e, 0, 0, 0)

            def body(b, last):
                row = Rows(b, last)

                def largest(n):
                    for k in range(NB):
                        dve.wait_ge(scores.sem, scores.level(b, n * NB + k + 1))
                        last_one = nc.vector.tensor_reduce(bank_max[:, k:k + 1],
                                                           ps_s[:, k, 0:min(BANK, KV - k * BANK)], AX.X, ALU.max)
                    last_one.then_inc(maxed.sem, 1)
                    dve.wait_ge(maxed.sem, maxed.level(b, n + 1))
                    nc.vector.tensor_reduce(neg_max[:, n % 2:n % 2 + 1], bank_max[:, :], AX.X, ALU.max,
                                            negate=True).then_inc(neg_ready.sem, 1)

                def invert(n):
                    dve.wait_ge(exped.sem, exped.level(b, 2 * n + 2))
                    nc.vector.tensor_tensor(row_sum[:, :], half_sum[:, n % 2, 0:1], half_sum[:, n % 2, 1:2],
                                            ALU.add).then_inc(summed.sem, 1)
                    dve.wait_ge(summed.sem, summed.level(b, n + 1))
                    nc.vector.reciprocal(inv_sum[:, n % 4:n % 4 + 1], row_sum[:, :]).then_inc(inverted.sem, 1)

                for n in range(N_STEPS + DRAIN):
                    if n < N_STEPS:
                        largest(n)
                    if 1 <= n <= N_STEPS:
                        invert(n - 1)
                    if n >= 4 and n % 2 == 0:
                        u = (n - 4) // 2
                        dve.wait_ge(inv_here.sem, inv_here.level(b, u + 1))
                        if u:
                            dve.wait_ge(out_lo.sem, out_lo.level(b, u))
                        nc.vector.tensor_tensor(out_n[:, :], ps_m[:, 0, :], inv_rows[:, :], ALU.mult
                                                ).then_inc(out_here.sem, 1)
                    for e in plans[last][n]:
                        entry(row, e, b, b + 1, b * G + e[2])

            rows(dve, body)

        @block.tensor
        def _(pe):
            def product(out, lhs, rhs, first, last):
                for n, (a, c) in enumerate(PARTS):
                    mm = nc.tensor.matmul(out, lhs(a), rhs(c), start=first and n == 0, stop=last and n == 2)
                return mm

            pe.wait_ge(cleared, 5)

            def ring(rows_, e, b_next, n):
                kind, m, _ = e
                if kind not in RING:
                    return
                bank = rows_.bank(e)
                out = ps_t[:, bank, :]
                if rows_.place(e) >= TB or rows_.at is not pro_at:
                    pe.wait_ge(*rows_.before(e))
                if kind == "xT":
                    pe.wait_ge(xn_ready.sem, xn_ready.level(b_next, 1))
                    for c in range(DC):
                        for t in range(QT):
                            mm = nc.tensor.transpose(out[:, (c * QT + t) * P:(c * QT + t + 1) * P],
                                                     xn[:, t, c * P:(c + 1) * P], eye[:, :])
                elif kind == "encT":
                    if m == 0:
                        pe.wait_ge(enc_in.sem, enc_in.level(b_next, 32))
                    for k, (tile, c) in enumerate(enc_block(m)):
                        top = P if tile < FULL else REST
                        at = k * P
                        mm = nc.tensor.transpose(out[:, at:at + top], enc[0:top, tile, c * P:(c + 1) * P],
                                                 eye[0:top, 0:top])
                elif kind == "q":
                    if m == 0:
                        pe.wait_ge(w_in_lo.sem, w_in_lo.level(n, 1))
                        if ("xT", 0, e[2]) in rows_.at:
                            pe.wait_ge(*rows_.empty(("xT", 0, e[2])))
                    for c in range(DC):
                        mm = product(out, lambda s: hT[:, s, c, m * P:(m + 1) * P],
                                     lambda s: w_in[:, s, c * HG * DH:(c + 1) * HG * DH], c == 0, c == DC - 1)
                elif kind == "kv":
                    if m == 0:
                        pe.wait_ge(w_in_lo.sem, w_in_lo.level(n, 2))
                    if m == 0 and ("encT", ENCJ - 1, e[2]) in rows_.at:
                        pe.wait_ge(*rows_.empty(("encT", ENCJ - 1, e[2])))
                    for i, tile in enumerate(kv_tiles(m)[0]):
                        top = P if tile < FULL else REST
                        for c in range(DC):
                            mm = product(out[0:top, i * 2 * DH:(i + 1) * 2 * DH],
                                         lambda s: encT[:, s, c, tile * P:tile * P + top],
                                         lambda s: w_in[:, s, WQ + c * 2 * DH:WQ + (c + 1) * 2 * DH],
                                         c == 0, c == DC - 1)
                elif kind == "qT":
                    pe.wait_ge(q_normed.sem, q_normed.level(n, 1))
                    for h in range(HG):
                        mm = nc.tensor.transpose(out[:, h * P:(h + 1) * P], qn[:, m, h * DH:(h + 1) * DH], eye[:, :])
                elif kind == "kT":
                    pe.wait_ge(k_normed.sem, k_normed.level(n, 1 if key_tiles[m][-1] < K_EARLY else 2))
                    for k, tile in enumerate(key_tiles[m]):
                        top = P if tile < FULL else REST
                        mm = nc.tensor.transpose(out[:, k * P:k * P + top], kn[0:top, tile, :], eye[0:top, 0:top])
                elif kind == "pT":
                    step, k = m // JOBS, m % JOBS
                    pe.wait_ge(exped.sem, exped.level(rows_.b, 2 * step + k // 2 + 1))
                    for i, tile in enumerate(key_tiles[k]):
                        top = P if tile < FULL else REST
                        mm = nc.tensor.transpose(out[0:top, i * P:(i + 1) * P],
                                                 probs[step % 2][:, tile * P:tile * P + top], eye[:, :])
                elif kind == "y":
                    pe.wait_ge(w_out_lo.sem, w_out_lo.level(rows_.b * G + m, 1))
                    pe.wait_ge(out_lo.sem, out_lo.level(rows_.b, (m + 1) * HG))
                    for t in range(QT):
                        for h in range(HG):
                            mm = product(out[:, t * D:(t + 1) * D], lambda s: oT[:, s, h, t * P:(t + 1) * P],
                                         lambda s: w_out[:, s, h * D:(h + 1) * D], h == 0, h == HG - 1)
                mm.then_inc(full.sem, 1)

            start = Start()
            for e in PROLOGUE:
                ring(start, e, 0, 0)

            def body(b, last):
                row = Rows(b, last)

                def score(n):
                    g, s = n // STEPS, n % STEPS
                    h, t, p = s // QT, s % QT, g % 2
                    for k in range(NB):
                        if s == 0 and k == 0:
                            pe.wait_ge(*(row.empty(("kT", JOBS - 1, g)) if g else (empty.sem, empty.level(b, 0))))
                        if n and k in (0, 2):
                            pe.wait_ge(exped.sem, exped.level(b, 2 * (n - 1) + k // 2 + 1))
                        a, z = k * BANK, min((k + 1) * BANK, COLS_EVEN)
                        mm = product(ps_s[:, k, 0:z - a], lambda s: qT[p][:, s, h, t * P:(t + 1) * P],
                                     lambda s: kT[p][:, s, a:z], True, True)
                        mm.then_inc(scores.sem, 1)

                def weigh(u, k):
                    if k == 0:
                        pe.wait_ge(*row.empty(("pT", (2 * u + 1) * JOBS + JOBS - 1, 0)))
                        if u:
                            pe.wait_ge(out_here.sem, out_here.level(b, u))
                    values = v[u // HG % 2]
                    for tile in key_tiles[k]:
                        top = P if tile < FULL else REST
                        product(ps_m[:, 0, :], lambda s: values[0:top, s, tile, :],
                                lambda s: pT[0:top, s, tile, :], tile == 0, tile == KT - 1)

                def spread(u):
                    pe.wait_ge(inverted.sem, inverted.level(b, 2 * u + 2))
                    for t in range(QT):
                        slot = (2 * u + t) % 4
                        mm = nc.tensor.matmul(ps_m[:, 1, t * P:(t + 1) * P],
                                              inv_sum[:, slot:slot + 1].broadcast_to([P, P]), eye[:, :],
                                              start=True, stop=True)
                    mm.then_inc(out_ready.sem, 1)

                for n in range(N_STEPS + DRAIN):
                    u = (n - 3) // 2
                    with_values = n >= 3 and n % 2 == 1
                    if n < N_STEPS:
                        score(n)
                    elif with_values:
                        for k in range(JOBS):
                            weigh(u, k)
                    for e in plans[last][n]:
                        if with_values and e[0] == "pT":
                            weigh(u, e[1] % JOBS)
                        ring(row, e, b + 1, b * G + e[2])
                    if with_values:
                        spread(u)

            rows(pe, body)


def bit_ffn(nc, x_sb, eye, half_power, w_gate, w_up, w_down, ln_weight):
    TT, D = x_sb.shape[1], x_sb.shape[2]
    I = w_gate.shape[0]
    DC, IC = D // P, I // P
    NB = I // BANK
    EPS, RMS_EPS = 1e-5, 1e-6
    TOP, BOTTOM = 127.0, -128.0
    ROUND = 1.5 * 2.0 ** 23
    K = D * I // P
    W = 3
    TILES = 4
    assert DC == 2 and IC == 8 and NB == 2 and TT == 8

    with ExitStack() as ctx:
        r = Room(nc, ctx, "bf")
        sb, ps, sem, counted = r.sb, r.ps, r.sem, r.counted
        w_raw = sb("w_raw", [P, W, K])
        w_abs = sb("w_abs", [P, K])
        w_clip = sb("w_clip", [P, W, K])
        w_sign = sb("w_sign", [P, W, K], BF16)
        wT = sb("wT", [P, W, K], BF16)
        abs_sum = sb("abs_sum", [P, W])
        ones = sb("ones", [P, P])
        eye_b = sb("eye_b", [P, P], BF16)
        w_mean = sb("w_mean", [P, W])
        w_scale = sb("w_scale", [P, W])
        ln_w = sb("ln_w", [P, I])
        stats = sb("stats", [P, TT, 6])
        mean_var = sb("mean_var", [P, TT, 2])
        var_eps = sb("var_eps", [P, TT])
        rstd = sb("rstd", [P, TT])
        xn = sb("xn", [P, TT, D])
        x_max = sb("x_max", [P, TT])
        x_inv = sb("x_inv", [P, TT])
        x_scale = sb("x_scale", [P, TT])
        gate_unit = sb("gate_unit", [P, TT])
        up_unit = sb("up_unit", [P, TT])
        xq = sb("xq", [P, TT, D], BF16)
        xqT = sb("xqT", [P, DC, TT * P], BF16)
        silu = [sb(f"silu{i}", [P, I]) for i in range(TILES)]
        h_squares = [sb(f"h_squares{i}", [P, I]) for i in range(TILES)]
        h = [sb(f"h{i}", [P, I]) for i in range(TILES)]
        hq = [sb(f"hq{i}", [P, I], BF16) for i in range(TILES)]
        hqT = [sb(f"hqT{i}", [P, IC, P], BF16) for i in range(TILES)]
        h_sq = sb("h_sq", [P, TILES])
        h_var = sb("h_var", [P, TILES])
        h_rstd = sb("h_rstd", [P, TILES])
        h_max = sb("h_max", [P, TILES])
        h_lim = sb("h_lim", [P, TILES])
        h_inv = sb("h_inv", [P, TILES])
        h_scale = sb("h_scale", [P, TILES])
        down_unit = sb("down_unit", [P, TILES])
        ps_g = ps("ps_g", [P, NB, BANK])
        ps_u = ps("ps_u", [P, NB, BANK])
        ps_t = ps("ps_t", [P, 2, 2 * BANK], BF16)
        ps_y = ps("ps_y", [P, 2, BANK])

        w_in = [sem(f"w_in{n}") for n in range(W)]
        ln_in = sem("ln_in")
        ones_set = sem("ones_set")
        abs_ready = sem("abs_ready")
        mean_ready = sem("mean_ready")
        prep = sem("prep")
        w_clipped = sem("w_clipped")
        w_signed = sem("w_signed")
        w_turned = sem("w_turned")
        w_here = sem("w_here")
        stat = sem("stat")
        var_ready = sem("var_ready")
        rstd_ready = sem("rstd_ready")
        x_rounded = sem("x_rounded")
        x_quantized = sem("x_quantized")
        x_turned = sem("x_turned")
        x_here = sem("x_here")
        N = TILES
        gu_ready = counted("gu_ready", N)
        silu_ready = counted("silu_ready", N)
        gated = counted("gated", N, before=1)
        squared = counted("squared", N)
        h_var_ready = counted("h_var_ready", N)
        h_rstd_ready = counted("h_rstd_ready", N)
        step = counted("step", 7 * N)
        rounded = counted("rounded", N)
        quantized = counted("quantized", N)
        turned = counted("turned", N)
        here = counted("here", N)
        y_ready = counted("y_ready", N)
        added = counted("added", N, before=1)

        block = ctx.enter_context(nc.Block())

        @block.sync
        def _(sp):
            for n, src in enumerate((w_gate, w_up, w_down)):
                sp.dma_start(w_raw[:, n, :].rearrange("p (a d) -> p a d", d=src.shape[1]),
                             src.rearrange("(a p) d -> p a d", p=P)).then_inc(w_in[n], 16)
            sp.dma_start(ln_w[:, :], ln_weight.rearrange("(a i) -> a i", a=1).broadcast_to([P, I])
                         ).then_inc(ln_in, 16)

        @block.gpsimd
        def _(pool):
            nc.gpsimd.memset(ones[:, :], 1.0).then_inc(ones_set, 1)
            nc.gpsimd.tensor_copy(eye_b[:, :], eye[:, :]).then_inc(ones_set, 1)
            pool.wait_ge(var_ready, 1)
            nc.gpsimd.tensor_tensor(rstd[:, :], var_eps[:, :], half_power[:, 0:TT], ALU.pow).then_inc(rstd_ready, 1)
            with pool.Fori(0, TT // TILES) as i:
                for k in range(TILES):
                    pool.wait_ge(h_var_ready.sem, h_var_ready.level(i, k + 1))
                    nc.gpsimd.tensor_tensor(h_rstd[:, k:k + 1], h_var[:, k:k + 1], half_power[:, 0:1], ALU.pow
                                            ).then_inc(h_rstd_ready.sem, 1)

        @block.scalar
        def _(act):
            for n in range(W):
                act.wait_ge(w_in[n], 16)
                if n:
                    act.wait_ge(abs_ready, n)
                nc.scalar.activation(w_abs[:, :], w_raw[:, n, :], ACT.Abs, accum_out=abs_sum[:, n:n + 1]
                                     ).then_inc(abs_ready, 1)
            act.wait_ge(x_rounded, 1)
            nc.scalar.activation(xq[:, :, :], xn[:, :, :], ACT.Copy, bias=-ROUND).then_inc(x_quantized, 1)
            for n in range(W):
                act.wait_ge(w_clipped, n + 1)
                nc.scalar.activation(w_sign[:, n, :], w_clip[:, n, :], ACT.Copy, bias=-ROUND).then_inc(w_signed, 1)
            with act.Fori(0, TT // TILES) as i:
                def gate(k):
                    act.wait_ge(gu_ready.sem, gu_ready.level(i, k + 1))
                    nc.scalar.activation(silu[k][:, :], ps_g[:, :, :].rearrange("p n m -> p (n m)"), ACT.Silu,
                                         scale=gate_unit[:, bass.ds(i * TILES + k, 1)]).then_inc(silu_ready.sem, 1)

                gate(0)
                for k in range(TILES + 1):
                    if k < TILES:
                        act.wait_ge(gated.sem, gated.level(i, k + 1))
                        nc.scalar.activation(h_squares[k][:, :], h[k][:, :], ACT.Square, accum_out=h_sq[:, k:k + 1]
                                             ).then_inc(squared.sem, 1)
                    if k + 1 < TILES:
                        gate(k + 1)
                    if k:
                        act.wait_ge(rounded.sem, rounded.level(i, k))
                        nc.scalar.activation(hq[k - 1][:, :], h[k - 1][:, :], ACT.Copy, bias=-ROUND
                                             ).then_inc(quantized.sem, 1)
                        act.wait_ge(turned.sem, turned.level(i, k))
                        nc.scalar.activation(hqT[k - 1][:, :, :].rearrange("p a b -> p (a b)"),
                                             ps_t[:, (k - 1) % 2, :], ACT.Copy).then_inc(here.sem, 1)

        @block.vector
        def _(dve):
            count = [0]

            def then(ins):
                count[0] += 1
                ins.then_inc(prep, 1)
                dve.wait_ge(prep, count[0])

            for t in range(TT):
                nc.vector.bn_stats(stats[:, t, :], x_sb[:, t, :]).then_inc(stat, 1)
            dve.wait_ge(stat, TT)
            for t in range(TT):
                nc.vector.bn_aggr(mean_var[:, t, :], stats[:, t, :]).then_inc(stat, 1)
            dve.wait_ge(stat, 2 * TT)
            nc.vector.tensor_scalar(var_eps[:, :], mean_var[:, :, 1], LN_EPS, None, ALU.add).then_inc(var_ready, 1)
            dve.wait_ge(rstd_ready, 1)
            for t in range(TT):
                last_one = nc.vector.tensor_scalar(xn[:, t, :], x_sb[:, t, :], mean_var[:, t, 0:1], rstd[:, t:t + 1],
                                                   ALU.subtract, ALU.mult)
            then(last_one)
            then(nc.vector.tensor_reduce(x_max[:, :], xn[:, :, :], AX.X, ALU.max, apply_absolute_value=True))
            then(nc.vector.tensor_scalar(x_max[:, :], x_max[:, :], EPS, None, ALU.max))
            then(nc.vector.reciprocal(x_inv[:, :], x_max[:, :]))
            then(nc.vector.tensor_scalar(x_scale[:, :], x_inv[:, :], TOP, None, ALU.mult))
            for t in range(TT):
                last_one = nc.vector.tensor_scalar(xn[:, t, :], xn[:, t, :], x_scale[:, t:t + 1], TOP,
                                                   ALU.mult, ALU.min)
            then(last_one)
            nc.vector.tensor_scalar(xn[:, :, :], xn[:, :, :], BOTTOM, ROUND, ALU.max, ALU.add).then_inc(x_rounded, 1)
            dve.wait_ge(mean_ready, 1)
            then(nc.vector.tensor_scalar(w_mean[:, :], ps_y[:, 0, 0:W], 1.0 / (D * I), EPS, ALU.mult, ALU.max))
            then(nc.vector.reciprocal(w_scale[:, :], w_mean[:, :]))
            for n in range(W):
                then(nc.vector.tensor_scalar(w_clip[:, n, :], w_raw[:, n, :], w_scale[:, n:n + 1], 1.0,
                                             ALU.mult, ALU.min))
                nc.vector.tensor_scalar(w_clip[:, n, :], w_clip[:, n, :], -1.0, ROUND, ALU.max, ALU.add
                                        ).then_inc(w_clipped, 1)
            then(nc.vector.tensor_scalar(gate_unit[:, :], x_max[:, :], w_mean[:, 0:1], 1.0 / TOP, ALU.mult, ALU.mult))
            then(nc.vector.tensor_scalar(up_unit[:, :], x_max[:, :], w_mean[:, 1:2], 1.0 / TOP, ALU.mult, ALU.mult))
            for c in range(DC):
                dve.wait_ge(x_turned, c + 1)
                nc.vector.tensor_copy(xqT[:, c, :], ps_t[:, c, :]).then_inc(x_here, 1)
            for m in range(2 * W):
                dve.wait_ge(w_turned, m + 1)
                nc.vector.tensor_copy(wT[:, m // 2, (m % 2) * I:(m % 2 + 1) * I], ps_t[:, m % 2, :]
                                      ).then_inc(w_here, 1)
            dve.wait_ge(ln_in, 16)
            dve.sem_inc(gated.sem, 1)
            dve.sem_inc(added.sem, 1)
            with dve.Fori(0, TT // TILES) as i:
                steps = [0]

                def then_inc_step(ins):
                    steps[0] += 1
                    ins.then_inc(step.sem, 1)

                def next_reads():
                    dve.wait_ge(step.sem, step.level(i, steps[0]))

                def gate(k):
                    dve.wait_ge(silu_ready.sem, silu_ready.level(i, k + 1))
                    nc.vector.scalar_tensor_tensor(h[k][:, :], ps_u[:, :, :].rearrange("p n m -> p (n m)"),
                                                   up_unit[:, bass.ds(i * TILES + k, 1)], silu[k][:, :],
                                                   ALU.mult, ALU.mult).then_inc(gated.sem, 1)

                def mean_square(k):
                    dve.wait_ge(squared.sem, squared.level(i, k + 1))
                    nc.vector.tensor_scalar(h_var[:, k:k + 1], h_sq[:, k:k + 1], 1.0 / I, RMS_EPS, ALU.mult, ALU.add
                                            ).then_inc(h_var_ready.sem, 1)

                def add(k):
                    dve.wait_ge(y_ready.sem, y_ready.level(i, k + 1))
                    row = x_sb[:, bass.ds(i * TILES + k, 1), :].rearrange("p a d -> p (a d)")
                    nc.vector.scalar_tensor_tensor(row, ps_y[:, k % 2, 0:D], down_unit[:, k:k + 1], row,
                                                   ALU.mult, ALU.add).then_inc(added.sem, 1)

                def norm(k):
                    dve.wait_ge(h_rstd_ready.sem, h_rstd_ready.level(i, k + 1))
                    then_inc_step(nc.vector.scalar_tensor_tensor(h[k][:, :], h[k][:, :], h_rstd[:, k:k + 1],
                                                                 ln_w[:, :], ALU.mult, ALU.mult))
                    next_reads()
                    then_inc_step(nc.vector.tensor_reduce(h_max[:, k:k + 1], h[k][:, :], AX.X, ALU.max,
                                                          apply_absolute_value=True))

                def quantize(k):
                    one = slice(k, k + 1)
                    next_reads()
                    then_inc_step(nc.vector.tensor_scalar(h_lim[:, one], h_max[:, one], EPS, None, ALU.max))
                    next_reads()
                    then_inc_step(nc.vector.reciprocal(h_inv[:, one], h_lim[:, one]))
                    next_reads()
                    then_inc_step(nc.vector.tensor_scalar(h_scale[:, one], h_inv[:, one], TOP, None, ALU.mult))
                    next_reads()
                    then_inc_step(nc.vector.tensor_scalar(h[k][:, :], h[k][:, :], h_scale[:, one], TOP,
                                                          ALU.mult, ALU.min))
                    next_reads()
                    nc.vector.tensor_scalar(h[k][:, :], h[k][:, :], BOTTOM, ROUND, ALU.max, ALU.add
                                            ).then_inc(rounded.sem, 1)
                    then_inc_step(nc.vector.tensor_scalar(down_unit[:, one], h_lim[:, one], w_mean[:, 2:3],
                                                          1.0 / TOP, ALU.mult, ALU.mult))
                    next_reads()

                for k in range(TILES + 2):
                    if k < TILES:
                        gate(k)
                    if 1 <= k <= TILES:
                        norm(k - 1)
                    if k < TILES:
                        mean_square(k)
                    if 1 <= k <= TILES:
                        quantize(k - 1)
                    if k >= 2:
                        add(k - 2)

        @block.tensor
        def _(pe):
            pe.wait_ge(ones_set, 2)
            pe.wait_ge(abs_ready, W)
            nc.tensor.matmul(ps_y[:, 0, 0:W], ones[:, :], abs_sum[:, :], start=True, stop=True
                             ).then_inc(mean_ready, 1)
            pe.wait_ge(x_quantized, 1)
            for c in range(DC):
                for t in range(TT):
                    mm = nc.tensor.transpose(ps_t[:, c, t * P:(t + 1) * P], xq[:, t, c * P:(c + 1) * P], eye_b[:, :])
                mm.then_inc(x_turned, 1)
            for m in range(2 * W):
                n, half = m // 2, m % 2
                pe.wait_ge(w_signed, n + 1)
                if m < 2:
                    pe.wait_ge(x_here, m + 1)
                else:
                    pe.wait_ge(w_here, m - 1)
                for k in range(IC):
                    if n < 2:
                        src = w_sign[:, n, :].rearrange("p (a d) -> p a d", d=D)[:, k, half * P:(half + 1) * P]
                    else:
                        chunk, o = (half * IC + k) // DC, k % DC
                        src = w_sign[:, n, :].rearrange("p (a i) -> p a i", i=I)[:, o, chunk * P:(chunk + 1) * P]
                    mm = nc.tensor.transpose(ps_t[:, m % 2, k * P:(k + 1) * P], src, eye_b[:, :])
                mm.then_inc(w_turned, 1)
            pe.wait_ge(w_here, 2 * W)
            with pe.Fori(0, TT // TILES) as i:
                def gate_up(k):
                    pe.wait_ge(gated.sem, gated.level(i, k))
                    for w, bank in ((0, ps_g), (1, ps_u)):
                        for n in range(NB):
                            for c in range(DC):
                                mm = nc.tensor.matmul(bank[:, n, :], xqT[:, c, bass.ds((i * TILES + k) * P, P)],
                                                      wT[:, w, c * I + n * BANK:c * I + (n + 1) * BANK],
                                                      start=c == 0, stop=c == DC - 1)
                    mm.then_inc(gu_ready.sem, 1)

                def down(k):
                    pe.wait_ge(quantized.sem, quantized.level(i, k + 1))
                    for c in range(IC):
                        mm = nc.tensor.transpose(ps_t[:, k % 2, c * P:(c + 1) * P], hq[k][:, c * P:(c + 1) * P],
                                                 eye_b[:, :])
                    mm.then_inc(turned.sem, 1)
                    pe.wait_ge(here.sem, here.level(i, k + 1))
                    pe.wait_ge(added.sem, added.level(i, max(k - 1, 0)))
                    for c in range(IC):
                        mm = nc.tensor.matmul(ps_y[:, k % 2, 0:D], hqT[k][:, c, :], wT[:, 2, c * D:(c + 1) * D],
                                              start=c == 0, stop=c == IC - 1)
                    mm.then_inc(y_ready.sem, 1)

                gate_up(0)
                gate_up(1)
                for k in range(TILES):
                    if k + 2 < TILES:
                        gate_up(k + 2)
                    down(k)


def build(nc, x, ctx_2048, wq, wk, wv, wo, gate_w, wg, wu, wd, cwg, cwu, cwd, wq1, wk1, wv1, wo1, qw, kw,
          w_gate, w_up, w_down, ln_weight, out):
    B, S, D = x.shape
    TT = B * S // P
    with ExitStack() as ctx:
        r = Room(nc, ctx, "all")
        x_sb = r.sb("x", [P, TT, D])
        eye = r.sb("eye", [P, P])
        half_power = r.sb("half_power", [P, 16])
        eye_zero = r.sem("eye_zero")
        stored = r.sem("stored")
        with nc.Block() as block:
            @block.gpsimd
            def _(pool):
                nc.gpsimd.memset(half_power[:, :], -0.5)
                nc.gpsimd.memset(eye[:, :], 0.0).then_inc(eye_zero, 1)
                pool.wait_ge(eye_zero, 1)
                nc.gpsimd.affine_select(out=eye[:, :], in_=eye[:, :], compare_op=ALU.not_equal, fill=1.0, base=0,
                                        pattern=[[-1, P]], channel_multiplier=1)
        cached_attention(nc, x_sb, eye, half_power, x, ctx_2048, wq, wk, wv, wo)
        experts(nc, x_sb, eye, half_power, gate_w, wg, wu, wd, cwg, cwu, cwd)
        grouped_attention(nc, x_sb, eye, half_power, ctx_2048, wq1, wk1, wv1, wo1, qw, kw)
        bit_ffn(nc, x_sb, eye, half_power, w_gate, w_up, w_down, ln_weight)
        with nc.Block() as block:
            @block.sync
            def _(sp):
                sp.dma_start(out.rearrange("b (t p) d -> p (b t) d", p=P), x_sb[:, :, :]).then_inc(stored, 16)
                sp.wait_ge(stored, 16)


_INS = ["x", "ctx_2048", "L0_xattn_wq", "L0_xattn_wk", "L0_xattn_wv", "L0_xattn_wo", "L0_ffn_gate_w",
        "L0_ffn_Wg", "L0_ffn_Wu", "L0_ffn_Wd", "L0_ffn_cWg", "L0_ffn_cWu", "L0_ffn_cWd",
        "L1_xattn_Wq", "L1_xattn_Wk", "L1_xattn_Wv", "L1_xattn_Wo", "L1_xattn_q_norm_w", "L1_xattn_k_norm_w",
        "L1_ffn_w_gate", "L1_ffn_w_up", "L1_ffn_w_down", "L1_ffn_ln_weight"]


def kernel(**inputs):
    import numpy as _np
    import concourse.bacc as _bacc
    from concourse import mybir as _mybir
    from concourse.bass_utils import run_bass_kernel_spmd as _run

    nc = _bacc.Bacc("TRN2", target_bir_lowering=False, num_devices=1)
    arrays, args = {}, []
    for name in _INS:
        a = _np.ascontiguousarray(inputs[name])
        arrays[f"in_{name}"] = a
        args.append(nc.dram_tensor(f"in_{name}", a.shape, _mybir.dt.from_np(a.dtype), kind="ExternalInput").ap())
    args.append(nc.dram_tensor("out_0", (4, 256, 256), _mybir.dt.float32, kind="ExternalOutput").ap())
    build(nc, *args)
    r = _run(nc, [arrays], core_ids=[0])
    return r.results[0]["out_0"]
```
